# Optimizing a Trainium2 kernel written in Bass

```python
import numpy as np
import jax
import jax.numpy as jnp

def _softmax(x, axis=-1):
    return jax.nn.softmax(x, axis=axis)

def _gelu(x):
    return jax.nn.gelu(x, approximate=True)

def _silu(x):
    return jax.nn.silu(x)

def _sigmoid(x):
    return jax.nn.sigmoid(x)

def _layernorm(x, axis=-1, eps=1e-05):
    m = jnp.mean(x, axis=axis, keepdims=True)
    v = jnp.var(x, axis=axis, keepdims=True)
    return (x - m) / jnp.sqrt(v + eps)

def _scatter_add(tgt, idx, src, axis=0):
    return tgt.at[idx].add(src)

def _segment_sum(src, seg, n):
    return jax.ops.segment_sum(src, seg, n)
kernel_name = 'mk_lm_tower_d2_tok_ids256_r4_2a8898'

def setup_inputs(seed: int=0):
    np.random.seed(seed)
    _w = jnp.asarray

    def _rec_inputs():
        import jax
        import jax.numpy as jnp
        _rk = jax.random.key(seed)
        x = jax.random.randint(jax.random.fold_in(_rk, 1), (128, 128), 0, 64, jnp.int32)
        return x
    x = _rec_inputs()

    def _L0_tok_setup():
        import jax, jax.numpy as jnp
        import numpy as np
        PRIME = 31
        VOCAB = 125000
        NGRAM_SIZES = (2, 3, 4)

        def _ngram_hash(byte_ids, n):
            T = byte_ids.shape[1]
            powers = PRIME ** jnp.arange(n - 1, -1, -1, dtype=jnp.int64) % VOCAB
            windows = jnp.stack([byte_ids[:, i:T - n + 1 + i] for i in range(n)], axis=-1)
            return (windows.astype(jnp.int64) * powers).sum(axis=-1) % VOCAB
        key = jax.random.key(seed)
        k0, k1, k2, k3 = jax.random.split(key, 4)
        byte_ids = jax.random.randint(k0, (8, 1024), 0, 64, dtype=jnp.int64)
        emb_2 = jax.random.normal(k1, (VOCAB, 64), dtype=jnp.float32)
        emb_3 = jax.random.normal(k2, (VOCAB, 64), dtype=jnp.float32)
        emb_4 = jax.random.normal(k3, (VOCAB, 64), dtype=jnp.float32)
        return {'byte_ids': byte_ids, 'emb_2': emb_2, 'emb_3': emb_3, 'emb_4': emb_4}
    _L0_tok_all = _L0_tok_setup()
    _L0_tok_in = {k: v for k, v in _L0_tok_all.items() if k in ('emb_2', 'emb_3', 'emb_4')}
    del _L0_tok_all

    def _L0_attn_setup():
        import jax, jax.numpy as jnp
        import numpy as np
        EMB_DIM = 64
        B, S = (8, 1024)
        key = jax.random.key(seed)
        ks = jax.random.split(key, 7)
        scale = EMB_DIM ** (-0.5)
        return {'x': jax.random.normal(ks[0], (B, S, EMB_DIM), dtype=jnp.float32), 'Wq': jax.random.normal(ks[1], (EMB_DIM, EMB_DIM), dtype=jnp.float32) * scale, 'bq': jnp.zeros((EMB_DIM,), dtype=jnp.float32), 'Wk': jax.random.normal(ks[2], (EMB_DIM, EMB_DIM), dtype=jnp.float32) * scale, 'bk': jnp.zeros((EMB_DIM,), dtype=jnp.float32), 'Wv': jax.random.normal(ks[3], (EMB_DIM, EMB_DIM), dtype=jnp.float32) * scale, 'bv': jnp.zeros((EMB_DIM,), dtype=jnp.float32)}
    _L0_attn_all = _L0_attn_setup()
    _L0_attn_in = {k: v for k, v in _L0_attn_all.items() if k in ('Wq', 'bq', 'Wk', 'bk', 'Wv', 'bv')}
    del _L0_attn_all

    def _L0_ffn_setup():
        import jax, jax.numpy as jnp
        import numpy as np
        B, T, IN_DIM = (64, 64, 64)
        HID, OUT_DIM = (128, 64)
        N_LAYERS, N_EXPERTS, N_SHARED = (2, 16, 1)
        key = jax.random.key(seed)
        ks = jax.random.split(key, 10)
        s = 0.02
        x = jax.random.normal(ks[0], (B, T, IN_DIM), dtype=jnp.float32)
        route_id = jax.random.randint(ks[1], (B,), 0, N_EXPERTS)
        Wi = jax.random.normal(ks[2], (HID, IN_DIM), dtype=jnp.float32) * s
        bi = jnp.zeros((HID,), dtype=jnp.float32)
        Wr = jax.random.normal(ks[3], (N_LAYERS, N_EXPERTS, HID, HID), dtype=jnp.float32) * s
        br = jax.random.normal(ks[4], (N_LAYERS, N_EXPERTS, HID), dtype=jnp.float32) * s
        Ws = jax.random.normal(ks[5], (N_LAYERS, N_SHARED, HID, HID), dtype=jnp.float32) * s
        bs = jax.random.normal(ks[6], (N_LAYERS, N_SHARED, HID), dtype=jnp.float32) * s
        Wo = jax.random.normal(ks[7], (OUT_DIM, HID), dtype=jnp.float32) * s
        bo = jnp.zeros((OUT_DIM,), dtype=jnp.float32)
        return {'x': x, 'route_id': route_id, 'Wi': Wi, 'bi': bi, 'Wr': Wr, 'br': br, 'Ws': Ws, 'bs': bs, 'Wo': Wo, 'bo': bo}
    _L0_ffn_all = _L0_ffn_setup()
    _L0_ffn_in = {k: v for k, v in _L0_ffn_all.items() if k in ('route_id', 'Wi', 'bi', 'Wr', 'br', 'Ws', 'bs', 'Wo', 'bo')}
    del _L0_ffn_all

    def _L1_attn_setup():
        import jax, jax.numpy as jnp
        import numpy as np
        DIM = 64
        HEADS = 4
        HEAD_DIM = DIM // HEADS
        MLP_HIDDEN = DIM * 3
        B, N = (8, 1024)
        EPS = 1e-05

        def _layernorm(x, g, b):
            mu = jnp.mean(x, axis=-1, keepdims=True)
            var = jnp.mean(jnp.square(x - mu), axis=-1, keepdims=True)
            return (x - mu) * jax.lax.rsqrt(var + EPS) * g + b
        key = jax.random.key(seed)
        ks = jax.random.split(key, 8)
        s = 0.02
        return {'x': jax.random.normal(ks[0], (B, N, DIM), dtype=jnp.float32), 'w_qkv': jax.random.normal(ks[1], (DIM, 3 * DIM), dtype=jnp.float32) * s, 'b_qkv': jnp.zeros((3 * DIM,), dtype=jnp.float32), 'norm_g': jnp.ones((DIM,), dtype=jnp.float32), 'norm_b': jnp.zeros((DIM,), dtype=jnp.float32), 'w_fc1': jax.random.normal(ks[2], (DIM, MLP_HIDDEN), dtype=jnp.float32) * s, 'b_fc1': jnp.zeros((MLP_HIDDEN,), dtype=jnp.float32), 'w_fc2': jax.random.normal(ks[3], (MLP_HIDDEN, DIM), dtype=jnp.float32) * s, 'b_fc2': jnp.zeros((DIM,), dtype=jnp.float32)}
    _L1_attn_all = _L1_attn_setup()
    _L1_attn_in = {k: v for k, v in _L1_attn_all.items() if k in ('w_qkv', 'b_qkv', 'norm_g', 'norm_b', 'w_fc1', 'b_fc1', 'w_fc2', 'b_fc2')}
    del _L1_attn_all

    def _L1_ffn_setup():
        import jax, jax.numpy as jnp
        import numpy as np
        DIM = 64
        HEADS = 8
        NUM_KEYS = 64
        NUM_KV = NUM_KEYS ** 2
        PK_TOPK = 16
        FINAL_TOPK = 16
        DIM_KEY = DIM // 2
        P = 2

        def _pk(x, Wq_pk, pk_keys):
            b, n, _ = x.shape
            q = (x @ Wq_pk).reshape(b, n, P, HEADS, DIM_KEY).transpose(2, 0, 1, 3, 4)
            sim = jnp.einsum('pbnhd,pkhd->pbnhk', q, pk_keys)
            scores, idx = jax.lax.top_k(sim, PK_TOPK)
            idx0 = idx[0]
            idx1 = idx[1] * NUM_KEYS
            index = (idx0[..., :, None] + idx1[..., None, :]).reshape(b, n, HEADS, PK_TOPK * PK_TOPK)
            score = (scores[0][..., :, None] + scores[1][..., None, :]).reshape(b, n, HEADS, PK_TOPK * PK_TOPK)
            final_scores, pk_idx = jax.lax.top_k(score, FINAL_TOPK)
            final_indices = jnp.take_along_axis(index, pk_idx, axis=-1)
            final_scores = jax.nn.softmax(final_scores, axis=-1)
            return (final_scores, final_indices)
        key = jax.random.key(seed)
        ks = jax.random.split(key, 7)
        b, n = (2, 256)
        std = 0.02
        x = jax.random.normal(ks[0], (b, n, DIM), dtype=jnp.float32)
        Wq_pk = jax.random.normal(ks[1], (DIM, P * HEADS * DIM_KEY), dtype=jnp.float32) * std
        pk_keys = jax.random.normal(ks[2], (P, NUM_KEYS, HEADS, DIM_KEY), dtype=jnp.float32) * std
        Wq = jax.random.normal(ks[3], (DIM, HEADS * DIM), dtype=jnp.float32) * std
        keys_table = jax.random.normal(ks[4], (NUM_KV * HEADS, DIM), dtype=jnp.float32) * std
        values_table = jax.random.normal(ks[5], (NUM_KV * HEADS, DIM), dtype=jnp.float32) * std
        Wo = jax.random.normal(ks[6], (DIM * HEADS, DIM), dtype=jnp.float32) * std
        return {'x': x, 'Wq_pk': Wq_pk, 'pk_keys': pk_keys, 'Wq': Wq, 'keys_table': keys_table, 'values_table': values_table, 'Wo': Wo}
    _L1_ffn_all = _L1_ffn_setup()
    _L1_ffn_in = {k: v for k, v in _L1_ffn_all.items() if k in ('Wq_pk', 'pk_keys', 'Wq', 'keys_table', 'values_table', 'Wo')}
    del _L1_ffn_all
    return {'x': x, 'L0_tok_emb_2': _L0_tok_in['emb_2'], 'L0_tok_emb_3': _L0_tok_in['emb_3'], 'L0_tok_emb_4': _L0_tok_in['emb_4'], 'L0_attn_Wq': _L0_attn_in['Wq'], 'L0_attn_bq': _L0_attn_in['bq'], 'L0_attn_Wk': _L0_attn_in['Wk'], 'L0_attn_bk': _L0_attn_in['bk'], 'L0_attn_Wv': _L0_attn_in['Wv'], 'L0_attn_bv': _L0_attn_in['bv'], 'L0_ffn_route_id': _L0_ffn_in['route_id'], 'L0_ffn_Wi': _L0_ffn_in['Wi'], 'L0_ffn_bi': _L0_ffn_in['bi'], 'L0_ffn_Wr': _L0_ffn_in['Wr'], 'L0_ffn_br': _L0_ffn_in['br'], 'L0_ffn_Ws': _L0_ffn_in['Ws'], 'L0_ffn_bs': _L0_ffn_in['bs'], 'L0_ffn_Wo': _L0_ffn_in['Wo'], 'L0_ffn_bo': _L0_ffn_in['bo'], 'L1_attn_w_qkv': _L1_attn_in['w_qkv'], 'L1_attn_b_qkv': _L1_attn_in['b_qkv'], 'L1_attn_norm_g': _L1_attn_in['norm_g'], 'L1_attn_norm_b': _L1_attn_in['norm_b'], 'L1_attn_w_fc1': _L1_attn_in['w_fc1'], 'L1_attn_b_fc1': _L1_attn_in['b_fc1'], 'L1_attn_w_fc2': _L1_attn_in['w_fc2'], 'L1_attn_b_fc2': _L1_attn_in['b_fc2'], 'L1_ffn_Wq_pk': _L1_ffn_in['Wq_pk'], 'L1_ffn_pk_keys': _L1_ffn_in['pk_keys'], 'L1_ffn_Wq': _L1_ffn_in['Wq'], 'L1_ffn_keys_table': _L1_ffn_in['keys_table'], 'L1_ffn_values_table': _L1_ffn_in['values_table'], 'L1_ffn_Wo': _L1_ffn_in['Wo']}

def reference(x, L0_tok_emb_2, L0_tok_emb_3, L0_tok_emb_4, L0_attn_Wq, L0_attn_bq, L0_attn_Wk, L0_attn_bk, L0_attn_Wv, L0_attn_bv, L0_ffn_route_id, L0_ffn_Wi, L0_ffn_bi, L0_ffn_Wr, L0_ffn_br, L0_ffn_Ws, L0_ffn_bs, L0_ffn_Wo, L0_ffn_bo, L1_attn_w_qkv, L1_attn_b_qkv, L1_attn_norm_g, L1_attn_norm_b, L1_attn_w_fc1, L1_attn_b_fc1, L1_attn_w_fc2, L1_attn_b_fc2, L1_ffn_Wq_pk, L1_ffn_pk_keys, L1_ffn_Wq, L1_ffn_keys_table, L1_ffn_values_table, L1_ffn_Wo):
    import jax
    import jax.numpy as jnp

    def _L0_tok_ref(byte_ids, emb_2, emb_3, emb_4):
        import jax, jax.numpy as jnp
        import numpy as np
        PRIME = 31
        VOCAB = 125000
        NGRAM_SIZES = (2, 3, 4)

        def _ngram_hash(byte_ids, n):
            T = byte_ids.shape[1]
            powers = PRIME ** jnp.arange(n - 1, -1, -1, dtype=jnp.int64) % VOCAB
            windows = jnp.stack([byte_ids[:, i:T - n + 1 + i] for i in range(n)], axis=-1)
            return (windows.astype(jnp.int64) * powers).sum(axis=-1) % VOCAB
        tables = {2: emb_2, 3: emb_3, 4: emb_4}
        B, T = byte_ids.shape
        D = emb_2.shape[1]
        out = jnp.zeros((B, T, D), dtype=emb_2.dtype)
        for n in NGRAM_SIZES:
            idx = _ngram_hash(byte_ids, n)
            gathered = tables[n][idx]
            out = out + jnp.pad(gathered, ((0, 0), (n - 1, 0), (0, 0)))
        return out / (len(NGRAM_SIZES) + 1)

    def _L0_attn_ref(x, Wq, bq, Wk, bk, Wv, bv):
        import jax, jax.numpy as jnp
        import numpy as np
        EMB_DIM = 64
        B, S = (8, 1024)
        q = jnp.einsum('bsd,ed->bse', x, Wq) + bq
        k = jnp.einsum('bsd,ed->bse', x, Wk) + bk
        v = jnp.einsum('bsd,ed->bse', x, Wv) + bv
        scores = jnp.einsum('bqd,bkd->bqk', q, k) * EMB_DIM ** (-0.5)
        attn = jax.nn.softmax(scores, axis=-1)
        return jnp.einsum('bqk,bkd->bqd', attn, v)

    def _L0_ffn_ref(x, route_id, Wi, bi, Wr, br, Ws, bs, Wo, bo):
        import jax, jax.numpy as jnp
        import numpy as np
        B, T, IN_DIM = (64, 64, 64)
        HID, OUT_DIM = (128, 64)
        N_LAYERS, N_EXPERTS, N_SHARED = (2, 16, 1)
        flat = x.reshape(-1, x.shape[-1])
        n_tok = flat.shape[0]
        route = jnp.repeat(route_id, n_tok // route_id.shape[0])
        h = jax.nn.relu(flat @ Wi.T + bi)
        n_layers, n_experts = (Wr.shape[0], Wr.shape[1])
        for l in range(n_layers):
            shared = (jnp.einsum('nd,shd->snh', h, Ws[l]) + bs[l][:, None, :]).mean(axis=0)
            routed = jnp.zeros_like(h)
            for e in range(n_experts):
                ye = h @ Wr[l, e].T + br[l, e]
                routed = routed + jnp.where((route == e)[:, None], ye, 0.0)
            h = jax.nn.relu(shared + routed + h)
        out = h @ Wo.T + bo
        return out.reshape(*x.shape[:-1], out.shape[-1])

    def _L1_attn_ref(x, w_qkv, b_qkv, norm_g, norm_b, w_fc1, b_fc1, w_fc2, b_fc2):
        import jax, jax.numpy as jnp
        import numpy as np
        DIM = 64
        HEADS = 4
        HEAD_DIM = DIM // HEADS
        MLP_HIDDEN = DIM * 3
        B, N = (8, 1024)
        EPS = 1e-05

        def _layernorm(x, g, b):
            mu = jnp.mean(x, axis=-1, keepdims=True)
            var = jnp.mean(jnp.square(x - mu), axis=-1, keepdims=True)
            return (x - mu) * jax.lax.rsqrt(var + EPS) * g + b
        Bx, Nx, C = x.shape
        scale = HEAD_DIM ** (-0.5)
        qkv = (x @ w_qkv + b_qkv).reshape(Bx, Nx, 3, HEADS, HEAD_DIM)
        qkv = jnp.transpose(qkv, (2, 0, 3, 1, 4))
        q, k, v = (qkv[0], qkv[1], qkv[2])
        k = k * scale
        attn = jnp.einsum('bhnd,bhne->bhde', k, v)
        attn = jax.nn.softmax(attn, axis=-1)
        xf = jnp.einsum('bhde,bhne->bhnd', attn, q)
        xf = jnp.transpose(xf, (0, 2, 1, 3)).reshape(Bx, Nx, C)
        x = x + xf
        h = _layernorm(x, norm_g, norm_b)
        h = jax.nn.gelu(h @ w_fc1 + b_fc1, approximate=False) @ w_fc2 + b_fc2
        return x + h

    def _L1_ffn_ref(x, Wq_pk, pk_keys, Wq, keys_table, values_table, Wo):
        import jax, jax.numpy as jnp
        import numpy as np
        DIM = 64
        HEADS = 8
        NUM_KEYS = 64
        NUM_KV = NUM_KEYS ** 2
        PK_TOPK = 16
        FINAL_TOPK = 16
        DIM_KEY = DIM // 2
        P = 2

        def _pk(x, Wq_pk, pk_keys):
            b, n, _ = x.shape
            q = (x @ Wq_pk).reshape(b, n, P, HEADS, DIM_KEY).transpose(2, 0, 1, 3, 4)
            sim = jnp.einsum('pbnhd,pkhd->pbnhk', q, pk_keys)
            scores, idx = jax.lax.top_k(sim, PK_TOPK)
            idx0 = idx[0]
            idx1 = idx[1] * NUM_KEYS
            index = (idx0[..., :, None] + idx1[..., None, :]).reshape(b, n, HEADS, PK_TOPK * PK_TOPK)
            score = (scores[0][..., :, None] + scores[1][..., None, :]).reshape(b, n, HEADS, PK_TOPK * PK_TOPK)
            final_scores, pk_idx = jax.lax.top_k(score, FINAL_TOPK)
            final_indices = jnp.take_along_axis(index, pk_idx, axis=-1)
            final_scores = jax.nn.softmax(final_scores, axis=-1)
            return (final_scores, final_indices)
        b, n, d = x.shape
        q = (x @ Wq).reshape(b, n, HEADS, DIM) * DIM ** (-0.5)
        kv_scores, indices = _pk(x, Wq_pk, pk_keys)
        offsets = jnp.arange(HEADS, dtype=indices.dtype) * NUM_KV
        ind = indices + offsets[None, None, :, None]
        k = jnp.einsum('bnhk,bnhkd->bnhd', kv_scores, keys_table[ind])
        v = jnp.einsum('bnhk,bnhkd->bnhd', kv_scores, values_table[ind])
        sim = jnp.einsum('bihd,bjhd->bhij', q, k)
        neg = -jnp.finfo(sim.dtype).max
        causal = jnp.tril(jnp.ones((n, n), dtype=bool))
        sim = jnp.where(causal, sim, neg)
        attn = jax.nn.softmax(sim, axis=-1)
        out = jnp.einsum('bhij,bjhd->bhid', attn, v)
        out = out.transpose(0, 2, 1, 3).reshape(b, n, HEADS * DIM)
        return out @ Wo
    h = _L0_tok_ref(x, L0_tok_emb_2, L0_tok_emb_3, L0_tok_emb_4)
    h = h + _L0_attn_ref(_layernorm(h, axis=-1), L0_attn_Wq, L0_attn_bq, L0_attn_Wk, L0_attn_bk, L0_attn_Wv, L0_attn_bv)
    h = h + _L0_ffn_ref(_layernorm(h, axis=-1), L0_ffn_route_id, L0_ffn_Wi, L0_ffn_bi, L0_ffn_Wr, L0_ffn_br, L0_ffn_Ws, L0_ffn_bs, L0_ffn_Wo, L0_ffn_bo)
    h = h + _L1_attn_ref(_layernorm(h, axis=-1), L1_attn_w_qkv, L1_attn_b_qkv, L1_attn_norm_g, L1_attn_norm_b, L1_attn_w_fc1, L1_attn_b_fc1, L1_attn_w_fc2, L1_attn_b_fc2)
    h = h + _L1_ffn_ref(_layernorm(h, axis=-1), L1_ffn_Wq_pk, L1_ffn_pk_keys, L1_ffn_Wq, L1_ffn_keys_table, L1_ffn_values_table, L1_ffn_Wo)
    return h

_drawn_inputs = setup_inputs


def setup_inputs(seed=0):
    import zlib

    import numpy as np

    out = dict(_drawn_inputs(seed))
    spreads = {'L0_attn_bq': (0.0, 0.1),
     'L0_attn_bk': (0.0, 2.0),
     'L0_attn_bv': (0.0, 0.1),
     'L0_ffn_bi': (0.0, 0.1),
     'L0_ffn_bo': (0.0, 0.1),
     'L1_attn_b_qkv': (0.0, 0.399),
     'L1_attn_norm_g': (1.0, 0.6),
     'L1_attn_norm_b': (0.0, 0.8),
     'L1_attn_b_fc1': (0.0, 0.715),
     'L1_attn_b_fc2': (0.0, 0.1)}
    factors = {'L0_ffn_Wr': 3.294,
     'L0_ffn_br': 5.543,
     'L0_ffn_Ws': 3.351,
     'L0_ffn_bs': 5.147,
     'L1_attn_w_fc1': 3.642,
     'L1_attn_w_fc2': 3.049,
     'L1_ffn_Wq_pk': 8.0,
     'L1_ffn_pk_keys': 8.0,
     'L1_ffn_Wq': 64.0,
     'L1_ffn_keys_table': 64.0,
     'L1_ffn_values_table': 8.0,
     'L1_ffn_Wo': 8.0}
    for name, (base, spread) in spreads.items():
        noise = np.random.default_rng([zlib.crc32(name.encode()), seed]).standard_normal(out[name].shape)
        drawn = base * np.exp(spread * noise) if base else spread * noise
        out[name] = jnp.asarray(drawn.astype(out[name].dtype))
    for name, factor in factors.items():
        out[name] = (out[name] * factor).astype(out[name].dtype)
    return out
```

```python
import numpy as np
import concourse.bass as bass
from concourse import mybir
from contextlib import ExitStack

ACT = mybir.ActivationFunctionType
ALU = mybir.AluOpType
AX = mybir.AxisListType
F32 = mybir.dt.float32
I32 = mybir.dt.int32
U32 = mybir.dt.uint32

SEQS, TOK, DIM = 128, 128, 64
GRAMS = (2, 3, 4)
PRIME, VOCAB = 31, 125000
HID, EXPERTS, GROUP = 128, 16, 2
ROUTES = SEQS // GROUP
EXPERT_ROW = 2 * HID + 2
HEAD_DIM = 16
MLP, MLP_HALF = 192, 96
HEADS, KEYS, KEY_DIM, TOP = 8, 64, 32, 16
EPS = 1e-5
MASKED = -1e30
REPLACED = -3.0e38
STAIRS = [(0, 1, 16), (1, 1, 8), (2, 1, 5), (3, 1, 4), (4, 1, 3), (5, 3, 2), (8, 8, 1)]
PAIRS = sum(n * m for _, n, m in STAIRS)
INDEX_COLS = 4

C_ID, C_CAUSAL, C_BLOCK, C_IOTA, C_GRAM, C_PART, C_EPS = 0, 128, 256, 320, 320 + PAIRS, 323 + PAIRS, 324 + PAIRS
C_COLS = 325 + PAIRS


def constants():
    c = np.zeros((128, C_COLS), np.float32)
    c[:, C_ID:C_ID + 128] = np.eye(128)
    c[:, C_CAUSAL:C_CAUSAL + 128] = np.triu(np.full((128, 128), MASKED), 1)
    head = np.arange(DIM) // HEAD_DIM
    c[:DIM, C_BLOCK:C_BLOCK + DIM] = np.where(head[:, None] == head[None, :], 0.0, MASKED)
    c[:, C_IOTA:C_IOTA + PAIRS] = np.arange(PAIRS)
    for n, g in enumerate(GRAMS):
        c[g - 1:, C_GRAM + n] = 1.0 / (len(GRAMS) + 1)
    c[:, C_PART] = np.arange(128)
    c[:, C_EPS] = EPS
    return c


def tower(nc, x, emb2, emb3, emb4, attn_w, wi_aug, route, wr, br, ws, bs, wo_ffn, bo, qkv_aug, norm_gb,
          fc1_aug, fc2, bfc2, wq_pk, pk_keys, wq, kv_table, wo, const, out):
    ctx = ExitStack()
    with ctx:
        def sb(name, shape, dt=F32):
            return ctx.enter_context(nc.sbuf_tensor(name, shape, dt))

        def pb(name):
            return ctx.enter_context(nc.psum_tensor(name, [128, 512], F32))

        def sem(name):
            return ctx.enter_context(nc.semaphore(name))

        expert_table = nc.dram_tensor("expert_table", ((EXPERTS + 1) * 128, EXPERT_ROW), F32).ap()

        C = sb("C", [128, C_COLS])
        ident = C[:, C_ID:C_ID + 128]
        causal = C[:, C_CAUSAL:C_CAUSAL + 128]
        block_mask = C[0:DIM, C_BLOCK:C_BLOCK + DIM]
        iota = C[:, C_IOTA:C_IOTA + PAIRS]
        eps = C[:, C_EPS:C_EPS + 1]
        attn_w_sb = sb("attn_w_sb", [DIM + 1, 3, DIM])
        wi_sb = sb("wi_sb", [DIM + 1, HID])
        wo_ffn_sb = sb("wo_ffn_sb", [HID, DIM])
        bo_sb = sb("bo_sb", [1, DIM])
        qkv_sb = sb("qkv_sb", [DIM + 1, 3 * DIM])
        gb_sb = sb("gb_sb", [DIM, 2])
        fc1_sb = sb("fc1_sb", [DIM + 1, MLP])
        fc2_sb = sb("fc2_sb", [MLP_HALF, 2, DIM])
        bfc2_sb = sb("bfc2_sb", [1, DIM])
        wq_pk_sb = sb("wq_pk_sb", [DIM, 2 * HEADS * KEY_DIM])
        keys_sb = sb("keys_sb", [128, 4, 4, KEYS])
        wq_sb = sb("wq_sb", [DIM, HEADS * DIM])
        wo_sb = sb("wo_sb", [DIM, HEADS, DIM])
        ones_row = sb("ones_row", [1, 128])

        ids = sb("ids", [SEQS, TOK], I32)
        idf = sb("idf", [SEQS, TOK])
        hashes = sb("hashes", [SEQS, 3, TOK])
        quot_i = sb("quot_i", [SEQS, 3, TOK], I32)
        quot = sb("quot", [SEQS, 3, TOK])
        index_all = sb("index_all", [TOK, SEQS + 2, INDEX_COLS], I32)
        route_i = sb("route_i", [128, ROUTES], I32)
        route_f = sb("route_f", [128, ROUTES])
        route_ok = sb("route_ok", [128, ROUTES])
        wr_sb = sb("wr_sb", [HID, 2, EXPERTS, HID])
        br_sb = sb("br_sb", [HID, 2, EXPERTS])
        ws_sb = sb("ws_sb", [HID, 2, HID])
        bs_sb = sb("bs_sb", [HID, 2])
        experts = sb("experts", [HID, EXPERTS + 1, EXPERT_ROW])

        index_cur = sb("index_cur", [TOK, INDEX_COLS], I32)
        emb = sb("emb", [TOK, 3, DIM])
        expert_w = sb("expert_w", [HID, EXPERT_ROW])
        stats = sb("stats", [TOK, 6])
        mv = sb("mv", [TOK, 2])
        std = sb("std", [TOK, 1])
        rstd = sb("rstd", [TOK, 1])
        h0 = sb("h0", [TOK, DIM])
        h1 = sb("h1", [TOK, DIM])
        h2 = sb("h2", [TOK, DIM])
        h3 = sb("h3", [TOK, DIM])
        xn = sb("xn", [TOK, DIM])
        xnT = sb("xnT", [DIM + 1, TOK])
        x2 = sb("x2", [TOK, DIM])
        x3 = sb("x3", [TOK, DIM])
        mlp_sum = sb("mlp_sum", [TOK, DIM])
        qkT = sb("qkT", [DIM, 2, TOK])
        v0 = sb("v0", [TOK, DIM])
        rowmax = sb("rowmax", [TOK, 1])
        negmax = sb("negmax", [TOK, 1])
        probs = sb("probs", [TOK, TOK])
        rowsum = sb("rowsum", [TOK, 1])
        rsum = sb("rsum", [TOK, 1])
        probsT = sb("probsT", [TOK, TOK])
        hidT = sb("hidT", [HID, 3, TOK])
        kv1 = sb("kv1", [TOK, 2 * DIM])
        q1T = sb("q1T", [DIM, TOK])
        mix = sb("mix", [DIM, DIM])
        mixn = sb("mixn", [DIM, DIM])
        mixT = sb("mixT", [DIM, DIM])
        geluT = sb("geluT", [MLP_HALF, 2, TOK])
        qpkT = sb("qpkT", [128, 4, TOK])
        sims = sb("sims", [TOK, 2 * HEADS, KEYS])

        top = sb("top", [TOK, 2, 2, TOP])
        pos = sb("pos", [TOK, 2, TOP], U32)
        rest = sb("rest", [TOK, 2, KEYS])
        pairs = sb("pairs", [TOK, 2, PAIRS])
        pairs_rest = sb("pairs_rest", [TOK, PAIRS])
        best = sb("best", [TOK, TOP])
        best_pos = sb("best_pos", [TOK, TOP], U32)
        onehot = sb("onehot", [TOK, TOP, PAIRS])
        negbest = sb("negbest", [TOK, 1])
        expbest = sb("expbest", [TOK, TOP])
        expsum = sb("expsum", [TOK, 1])
        rexp = sb("rexp", [TOK, 1])
        weight = sb("weight", [TOK, HEADS, TOP])
        row_index = sb("row_index", [TOK, HEADS, TOP], I32)

        rows = sb("rows", [TOK, HEADS, TOP, 2 * DIM])
        diag = sb("diag", [TOK, 2, TOP, TOK])
        h3_cur = sb("h3_cur", [TOK, DIM])
        x4T_cur = sb("x4T_cur", [DIM, TOK])
        x4T = xnT[0:DIM, :]
        qhT = sb("qhT", [DIM, TOK])
        kvT = sb("kvT", [2 * DIM, TOK])
        v_rows = sb("v_rows", [TOK, DIM])
        b_max = sb("b_max", [TOK, 1])
        b_neg = sb("b_neg", [TOK, 1])
        b_probs = sb("b_probs", [TOK, TOK])
        b_sum = sb("b_sum", [TOK, 1])
        b_rsum = sb("b_rsum", [TOK, 1])
        b_norm = sb("b_norm", [TOK, TOK])
        b_probsT = sb("b_probsT", [TOK, TOK])
        headT = sb("headT", [DIM, TOK])
        out_sb = sb("out_sb", [TOK, DIM])

        front_a, front_b = pb("front_a"), pb("front_b")
        sim_ps = [pb("sim_ps0"), pb("sim_ps1")]
        kv_ps = pb("kv_ps")
        score_ps = pb("score_ps")
        turn_ps = pb("turn_ps")
        y_ps = pb("y_ps")

        loaded = sem("loaded")
        ids_loaded = sem("ids_loaded")
        experts_loaded = sem("experts_loaded")
        const_loaded = sem("const_loaded")
        consts_set = sem("consts_set")
        keys_cleared = sem("keys_cleared")
        hashed = sem("hashed")
        hashT_ready = sem("hashT_ready")
        experts_ready = sem("experts_ready")
        experts_stored = sem("experts_stored")
        cur_ready = sem("cur_ready")
        emb_loaded = sem("emb_loaded")
        expert_arrived = sem("expert_arrived")
        emb_used = sem("emb_used")
        held = sem("held")
        var_ready, std_ready = sem("var_ready"), sem("std_ready")
        xn_ready, xnT_ps_ready, xnT_ready = sem("xn_ready"), sem("xnT_ps_ready"), sem("xnT_ready")
        qkv_ps_ready, qkv_ready = sem("qkv_ps_ready"), sem("qkv_ready")
        scores_ready, negmax_ready, probs_ready = sem("scores_ready"), sem("negmax_ready"), sem("probs_ready")
        pT_ps_ready, pT_ready, attn_ps_ready = sem("pT_ps_ready"), sem("pT_ready"), sem("attn_ps_ready")
        hid_ps_ready, hid_ready, ffn_ps_ready = sem("hid_ps_ready"), sem("hid_ready"), sem("ffn_ps_ready")
        qkv1_ps_ready, qkv1_ready = sem("qkv1_ps_ready"), sem("qkv1_ready")
        mix_ps_ready, mixmax_ready, mix_ready = sem("mix_ps_ready"), sem("mixmax_ready"), sem("mix_ready")
        mixn_ready, mixT_ps_ready, mixT_ready = sem("mixn_ready"), sem("mixT_ps_ready"), sem("mixT_ready")
        xf_ps_ready = sem("xf_ps_ready")
        fc1_ps_ready, gelu_ready, mlp_ps_ready = sem("fc1_ps_ready"), sem("gelu_ready"), sem("mlp_ps_ready")
        qpk_ps_ready, qpk_ready = sem("qpk_ps_ready"), sem("qpk_ready")
        sim_ps_ready, sims_ready = sem("sim_ps_ready"), sem("sims_ready")
        best_ready, expbest_ready = sem("best_ready"), sem("expbest_ready")
        weight_ready, index_ready = sem("weight_ready"), sem("index_ready")
        rows_loaded = [sem(f"rows_loaded{h}") for h in range(HEADS)]
        diag_ready, kv_done, qhT_ready = sem("diag_ready"), sem("kv_done"), sem("qhT_ready")
        kvT_ready, b_scores_ready, v_ready = sem("kvT_ready"), sem("b_scores_ready"), sem("v_ready")
        b_neg_ready, b_probs_ready, b_norm_ready = sem("b_neg_ready"), sem("b_probs_ready"), sem("b_norm_ready")
        b_pT_ps_ready, b_pT_ready = sem("b_pT_ps_ready"), sem("b_pT_ready")
        headT_ps_ready, headT_ready, y_ready = sem("headT_ps_ready"), sem("headT_ready"), sem("y_ready")
        carried, out_ready, out_stored = sem("carried"), sem("out_ready"), sem("out_stored")

        def wait(eng, semaphore, count):
            eng.wait_ge(semaphore, count)
            if not isinstance(count, int):
                eng.sem_inc(held, 1)

        LAYER_NORMS = 5
        SMALL_LOADS = [(attn_w_sb, attn_w), (wi_sb, wi_aug), (wo_ffn_sb, wo_ffn), (bo_sb, bo), (qkv_sb, qkv_aug),
                       (gb_sb, norm_gb), (fc1_sb, fc1_aug), (fc2_sb, fc2), (bfc2_sb, bfc2), (wq_pk_sb, wq_pk),
                       (wq_sb, wq), (wo_sb, wo)]
        N_LOADED = 16 * (len(SMALL_LOADS) + 2 * HEADS)

        block = ctx.enter_context(nc.Block())

        @block.sync
        def _(sp):
            sp.dma_start(C[:, :], const).then_inc(const_loaded, 16)
            sp.dma_start(ids[:, :], x).then_inc(ids_loaded, 16)
            sp.dma_start(route_i[:, :], route.partition_broadcast(128)).then_inc(ids_loaded, 16)
            for dst, src in ((wr_sb, wr), (br_sb, br), (ws_sb, ws), (bs_sb, bs)):
                sp.dma_start(dst[:], src).then_inc(experts_loaded, 16)
            for dst, src in SMALL_LOADS:
                sp.dma_start(dst[:], src).then_inc(loaded, 16)
            sp.wait_ge(keys_cleared, 1)
            for half in range(2):
                for h in range(HEADS):
                    q = h % 4
                    sp.dma_start(keys_sb[q * KEY_DIM:(q + 1) * KEY_DIM, half * 2 + h // 4, q, :],
                                 pk_keys[half, h, :, :]).then_inc(loaded, 16)
            sp.wait_ge(experts_ready, 1)
            sp.dma_start(expert_table.rearrange("(e p) c -> p e c", p=128), experts[:]).then_inc(experts_stored, 16)

            def store(s):
                wait(sp, out_ready, s + 1)
                sp.dma_start(out[bass.ds(s, 1), :, :].rearrange("a t d -> t (a d)"), out_sb[:, :]).then_inc(out_stored, 16)

            with sp.Fori(0, SEQS) as s:
                store(s)
            sp.wait_ge(out_stored, 16 * SEQS)
            sp.wait_ge(experts_stored, 16)

        @block.gpsimd
        def _(pool):
            def gather(dst, table, index):
                return nc.gpsimd.indirect_dma_start(out=dst, out_offset=None, in_=table,
                                                    in_offset=bass.IndirectOffsetOnAxis(ap=index, axis=0))

            def token_rows(s, first=False):
                wait(pool, cur_ready, s + 1)
                if not first:
                    wait(pool, emb_used, s)
                    wait(pool, ffn_ps_ready, s)
                for n, table in enumerate((emb2, emb3, emb4)):
                    gather(emb[:, n, :], table, index_cur[:, n:n + 1]).then_inc(emb_loaded, 16)
                gather(expert_w[:, :], expert_table, index_cur[:, 3:4]).then_inc(expert_arrived, 16)

            def head_rows(s, h):
                wait(pool, index_ready, s * HEADS + h + 1)
                for k in range(TOP):
                    gather(rows[:, h, k, :], kv_table, row_index[:, h, k:k + 1]).then_inc(rows_loaded[h], 16)

            pool.wait_ge(experts_stored, 16)
            token_rows(0, first=True)
            token_rows(1)
            for h in range(HEADS):
                head_rows(0, h)
            with pool.Fori(0, SEQS - 1) as i:
                token_rows(i + 2)
                for h in range(HEADS):
                    wait(pool, kv_done, i * HEADS + h + 1)
                    head_rows(i + 1, h)
            pool.wait_ge(emb_loaded, 48 * (SEQS + 1))
            pool.wait_ge(expert_arrived, 16 * (SEQS + 1))

        @block.scalar
        def _(act):
            def copy(dst, src):
                return nc.scalar.activation(dst, src, ACT.Copy)

            def layer_std(s, n):
                wait(act, var_ready, s * LAYER_NORMS + n + 1)
                nc.scalar.activation(std[:, :], mv[:, 1:2], ACT.Sqrt, bias=eps).then_inc(std_ready, 1)

            def transposed(s, n):
                wait(act, xnT_ps_ready, s * LAYER_NORMS + n + 1)
                copy(xnT[0:DIM, :], front_a[0:DIM, 0:TOK]).then_inc(xnT_ready, 1)

            def front(s):
                layer_std(s, 0)
                transposed(s, 0)
                wait(act, qkv_ps_ready, s + 1)
                copy(qkT[:, :, :], front_b[0:DIM, 0:2 * TOK].rearrange("p (a t) -> p a t", a=2))
                copy(v0[:, :], front_b[:, 256:256 + DIM]).then_inc(qkv_ready, 1)
                wait(act, negmax_ready, s + 1)
                nc.scalar.activation(probs[:, :], front_a[:, 128:256], ACT.Exp, bias=negmax[:, :],
                                     scale=DIM ** -0.5, accum_out=rowsum[:, :]).then_inc(probs_ready, 1)
                wait(act, pT_ps_ready, s + 1)
                copy(probsT[:, :], front_a[:, 256:384]).then_inc(pT_ready, 1)
                layer_std(s, 1)
                transposed(s, 1)
                for n in range(3):
                    wait(act, hid_ps_ready, 3 * s + n + 1)
                    bias = {} if n == 0 else {"bias": expert_w[:, 2 * HID + n - 1:2 * HID + n]}
                    nc.scalar.activation(hidT[:, n, :], front_b[:, 128 * n:128 * n + 128], ACT.Relu, **bias).then_inc(hid_ready, 1)
                layer_std(s, 2)
                transposed(s, 2)
                wait(act, qkv1_ps_ready, s + 1)
                copy(kv1[:, :], front_b[:, 0:128])
                copy(q1T[:, :], front_b[0:DIM, 128:256]).then_inc(qkv1_ready, 1)
                wait(act, mixmax_ready, s + 1)
                nc.scalar.activation(mix[:, :], front_a[0:DIM, 128:128 + DIM], ACT.Exp, bias=negmax[0:DIM, :],
                                     scale=HEAD_DIM ** -0.5, accum_out=rowsum[0:DIM, :]).then_inc(mix_ready, 1)
                wait(act, mixT_ps_ready, s + 1)
                copy(mixT[:, :], front_a[0:DIM, 256:256 + DIM]).then_inc(mixT_ready, 1)
                layer_std(s, 3)
                wait(act, xnT_ps_ready, s * LAYER_NORMS + 4)
                nc.scalar.activation(xnT[0:DIM, :], front_a[0:DIM, 0:TOK], ACT.Identity, bias=gb_sb[:, 1:2],
                                     scale=gb_sb[:, 0:1]).then_inc(xnT_ready, 1)
                wait(act, fc1_ps_ready, s + 1)
                nc.scalar.activation(geluT[:, :, :], front_b[0:MLP_HALF, 0:256].rearrange("p (a t) -> p a t", a=2),
                                     ACT.Gelu).then_inc(gelu_ready, 1)
                layer_std(s, 4)
                transposed(s, 4)
                wait(act, qpk_ps_ready, s + 1)
                copy(qpkT[:, :, :], front_b[:, :].rearrange("p (a t) -> p a t", a=4)).then_inc(qpk_ready, 1)
                for b in range(2):
                    wait(act, sim_ps_ready, 2 * s + b + 1)
                    copy(sims[:, 8 * b:8 * b + 8, :], sim_ps[b][:, :].rearrange("p (a t) -> p a t", a=8)).then_inc(sims_ready, 1)

            def select(s, h):
                n = s * HEADS + h
                wait(act, best_ready, n + 1)
                nc.scalar.activation(expbest[:, :], best[:, :], ACT.Exp, bias=negbest[:, :],
                                     accum_out=expsum[:, :]).then_inc(expbest_ready, 1)

            def diagonals(s, h):
                wait(act, weight_ready, s * HEADS + h + 1)
                for k in range(TOP):
                    last = nc.scalar.activation(diag[:, h % 2, k, :], ident, ACT.Copy, scale=weight[:, h, k:k + 1])
                last.then_inc(diag_ready, 1)

            def back(s, h):
                n = s * HEADS + h
                wait(act, kv_done, n + 1)
                copy(kvT[:, :], kv_ps[:, 0:TOK])
                copy(qhT[:, :], kv_ps[0:DIM, 128:256]).then_inc(kvT_ready, 1)
                if h + 1 < HEADS:
                    diagonals(s, h + 1)
                wait(act, v_ready, n + 1)
                copy(v_rows[:, :], turn_ps[:, 0:DIM])
                wait(act, b_neg_ready, n + 1)
                nc.scalar.activation(b_probs[:, :], score_ps[:, 0:TOK], ACT.Exp, bias=b_neg[:, :],
                                     scale=DIM ** -0.5, accum_out=b_sum[:, :]).then_inc(b_probs_ready, 1)

            act.wait_ge(const_loaded, 16)
            act.wait_ge(loaded, N_LOADED)
            front(0)
            for h in range(HEADS):
                select(0, h)
            with act.Fori(0, SEQS - 1) as i:
                diagonals(i, 0)
                front(i + 1)
                for h in range(HEADS):
                    back(i, h)
                    select(i + 1, h)
            diagonals(SEQS - 1, 0)
            for h in range(HEADS):
                back(SEQS - 1, h)

        @block.vector
        def _(dve):
            v = nc.vector

            def layer_norm(s, n, src, dst):
                dve.drain()
                v.bn_stats(stats[:, :], src)
                dve.drain()
                v.bn_aggr(mv[:, :], stats[:, :]).then_inc(var_ready, 1)
                wait(dve, std_ready, s * LAYER_NORMS + n + 1)
                v.reciprocal(rstd[:, :], std[:, :])
                dve.drain()
                v.tensor_scalar(dst, src, mv[:, 0:1], rstd[:, :], ALU.subtract, ALU.mult).then_inc(xn_ready, 1)

            def negated_max(scores, high, low, scale):
                v.reduce_max(high, scores, AX.X)
                dve.drain()
                return v.tensor_scalar(low, high, -scale, None, ALU.mult)

            def front(s):
                wait(dve, emb_loaded, 48 * s + 48)
                wait(dve, expert_arrived, 16 * s + 16)
                v.tensor_copy(index_cur[:, :], index_all[:, bass.ds(s + 1, 1), :].rearrange("p a c -> p (a c)")).then_inc(cur_ready, 1)
                v.tensor_scalar(h0[:, :], emb[:, 0, :], C[:, C_GRAM:C_GRAM + 1], None, ALU.mult)
                dve.drain()
                v.scalar_tensor_tensor(h0[:, :], emb[:, 1, :], C[:, C_GRAM + 1:C_GRAM + 2], h0[:, :], ALU.mult, ALU.add)
                dve.drain()
                v.scalar_tensor_tensor(h0[:, :], emb[:, 2, :], C[:, C_GRAM + 2:C_GRAM + 3], h0[:, :], ALU.mult, ALU.add).then_inc(emb_used, 1)
                layer_norm(s, 0, h0[:, :], xn[:, :])
                wait(dve, scores_ready, s + 1)
                negated_max(front_a[:, 128:256], rowmax[:, :], negmax[:, :], DIM ** -0.5).then_inc(negmax_ready, 1)
                wait(dve, probs_ready, s + 1)
                v.reciprocal(rsum[:, :], rowsum[:, :])
                dve.drain()
                wait(dve, attn_ps_ready, s + 1)
                v.scalar_tensor_tensor(h1[:, :], front_b[:, 384:384 + DIM], rsum[:, :], h0[:, :], ALU.mult, ALU.add)
                layer_norm(s, 1, h1[:, :], xn[:, :])
                wait(dve, ffn_ps_ready, s + 1)
                v.tensor_tensor(h2[:, :], h1[:, :], front_a[:, 384:384 + DIM], ALU.add)
                layer_norm(s, 2, h2[:, :], x2[:, :])
                wait(dve, mix_ps_ready, s + 1)
                negated_max(front_a[0:DIM, 128:128 + DIM], rowmax[0:DIM, :], negmax[0:DIM, :], HEAD_DIM ** -0.5).then_inc(mixmax_ready, 1)
                wait(dve, mix_ready, s + 1)
                v.reciprocal(rsum[0:DIM, :], rowsum[0:DIM, :])
                dve.drain()
                v.tensor_scalar(mixn[:, :], mix[:, :], rsum[0:DIM, :], None, ALU.mult).then_inc(mixn_ready, 1)
                wait(dve, xf_ps_ready, s + 1)
                v.tensor_tensor(x3[:, :], x2[:, :], front_a[:, 384:384 + DIM], ALU.add)
                layer_norm(s, 3, x3[:, :], xn[:, :])
                wait(dve, mlp_ps_ready, s + 1)
                v.tensor_tensor(mlp_sum[:, :], x3[:, :], front_b[:, 384:384 + DIM], ALU.add)
                dve.drain()
                v.tensor_tensor(h3[:, :], h2[:, :], mlp_sum[:, :], ALU.add)
                layer_norm(s, 4, h3[:, :], xn[:, :])
                wait(dve, sims_ready, 2 * s + 2)

            def select(s, h):
                n = s * HEADS + h
                part = [sims[:, h, :], sims[:, HEADS + h, :]]
                for a in range(2):
                    v.max(top[:, a, 0, 0:8], part[a])
                dve.drain()
                for a in range(2):
                    v.max_index(pos[:, a, 0:8], top[:, a, 0, 0:8], part[a])
                    v.match_replace(rest[:, a, :], top[:, a, 0, 0:8], part[a], REPLACED)
                dve.drain()
                for a in range(2):
                    v.max(top[:, a, 0, 8:16], rest[:, a, :])
                dve.drain()
                for a in range(2):
                    v.max_index(pos[:, a, 8:16], top[:, a, 0, 8:16], rest[:, a, :])
                dve.drain()
                v.tensor_scalar(top[:, 0, 1, :], pos[:, 0, :], float(h * KEYS * KEYS), None, ALU.add)
                v.tensor_scalar(top[:, 1, 1, :], pos[:, 1, :], float(KEYS), None, ALU.mult)
                dve.drain()
                at = 0
                for i0, ni, nj in STAIRS:
                    v.tensor_tensor(pairs[:, :, at:at + ni * nj].rearrange("p a (i j) -> p a i j", i=ni),
                                    top[:, 0, :, i0:i0 + ni].unsqueeze(3).broadcast_to([TOK, 2, ni, nj]),
                                    top[:, 1, :, 0:nj].unsqueeze(2).broadcast_to([TOK, 2, ni, nj]), ALU.add)
                    at += ni * nj
                dve.drain()
                v.max(best[:, 0:8], pairs[:, 0, :])
                dve.drain()
                v.tensor_scalar(negbest[:, :], best[:, 0:1], -1.0, None, ALU.mult)
                v.max_index(best_pos[:, 0:8], best[:, 0:8], pairs[:, 0, :])
                v.match_replace(pairs_rest[:, :], best[:, 0:8], pairs[:, 0, :], REPLACED)
                dve.drain()
                v.max(best[:, 8:16], pairs_rest[:, :]).then_inc(best_ready, 1)
                dve.drain()
                v.max_index(best_pos[:, 8:16], best[:, 8:16], pairs_rest[:, :])
                dve.drain()
                v.tensor_tensor(onehot[:, :, :], best_pos[:, :].unsqueeze(2).broadcast_to([TOK, TOP, PAIRS]),
                                iota.unsqueeze(1).broadcast_to([TOK, TOP, PAIRS]), ALU.is_equal)
                dve.drain()
                v.tensor_tensor(onehot[:, :, :], onehot[:, :, :], pairs[:, 1, :].unsqueeze(1).broadcast_to([TOK, TOP, PAIRS]), ALU.mult)
                dve.drain()
                with nc.allow_low_precision(reason="one row number and zeros: exact"):
                    v.tensor_reduce(row_index[:, h, :], onehot[:, :, :], AX.X, ALU.add).then_inc(index_ready, 1)
                wait(dve, expbest_ready, n + 1)
                v.reciprocal(rexp[:, :], expsum[:, :])
                dve.drain()
                v.tensor_scalar(weight[:, h, :], expbest[:, :], rexp[:, :], None, ALU.mult).then_inc(weight_ready, 1)

            def back(s, h):
                n = s * HEADS + h
                wait(dve, b_scores_ready, n + 1)
                negated_max(score_ps[:, 0:TOK], b_max[:, :], b_neg[:, :], DIM ** -0.5).then_inc(b_neg_ready, 1)
                wait(dve, b_probs_ready, n + 1)
                v.reciprocal(b_rsum[:, :], b_sum[:, :])
                dve.drain()
                v.tensor_scalar(b_norm[:, :], b_probs[:, :], b_rsum[:, :], None, ALU.mult).then_inc(b_norm_ready, 1)
                wait(dve, b_pT_ps_ready, n + 1)
                v.tensor_copy(b_probsT[:, :], turn_ps[:, 128:256]).then_inc(b_pT_ready, 1)
                wait(dve, headT_ps_ready, n + 1)
                v.tensor_copy(headT[:, :], turn_ps[0:DIM, 256:384]).then_inc(headT_ready, 1)

            def finish(s):
                wait(dve, y_ready, s + 1)
                v.tensor_tensor(out_sb[:, :], h3_cur[:, :], y_ps[:, 0:DIM], ALU.add).then_inc(out_ready, 1)

            def carry():
                v.tensor_copy(h3_cur[:, :], h3[:, :])
                v.tensor_copy(x4T_cur[:, :], x4T).then_inc(carried, 1)

            v.memset(keys_sb[:], 0.0).then_inc(keys_cleared, 1)
            v.memset(ones_row[:, :], 1.0)
            v.memset(xnT[DIM:DIM + 1, :], 1.0).then_inc(consts_set, 1)
            v.memset(hashes[:], 0.0)
            v.memset(index_all[:], 0)
            dve.wait_ge(ids_loaded, 32)
            v.tensor_copy(idf[:, :], ids[:, :])
            v.tensor_copy(route_f[:, :], route_i[:, :])
            dve.drain()
            for n, g in enumerate(GRAMS):
                back_by = g - 1
                newer = idf[:, back_by:] if n == 0 else hashes[:, n - 1, back_by:]
                v.scalar_tensor_tensor(hashes[:, n, back_by:], idf[:, 0:TOK - back_by], float(PRIME ** back_by % VOCAB),
                                       newer, ALU.mult, ALU.add)
                dve.drain()
            v.tensor_scalar(quot_i[:], hashes[:], 1.0 / VOCAB, None, ALU.mult)
            dve.drain()
            v.tensor_copy(quot[:], quot_i[:])
            dve.drain()
            v.scalar_tensor_tensor(hashes[:], quot[:], float(-VOCAB), hashes[:], ALU.mult, ALU.add)
            dve.drain()
            v.tensor_scalar(quot[:], hashes[:], 0.0, float(VOCAB), ALU.is_lt, ALU.mult)
            dve.drain()
            v.tensor_tensor(hashes[:], hashes[:], quot[:], ALU.add)
            dve.drain()
            v.tensor_scalar(quot[:], hashes[:], float(VOCAB), float(-VOCAB), ALU.is_ge, ALU.mult)
            dve.drain()
            v.tensor_tensor(hashes[:], hashes[:], quot[:], ALU.add).then_inc(hashed, 1)
            dve.wait_ge(const_loaded, 16)
            v.tensor_scalar(route_ok[:, :], route_f[:, :], 0.0, None, ALU.is_ge)
            dve.drain()
            v.scalar_tensor_tensor(route_ok[:, :], route_f[:, :], float(EXPERTS - 1), route_ok[:, :], ALU.is_le, ALU.mult)
            dve.drain()
            v.scalar_tensor_tensor(route_f[:, :], route_f[:, :], float(-EXPERTS), route_ok[:, :], ALU.add, ALU.mult)
            dve.drain()
            v.tensor_scalar(route_f[:, :], route_f[:, :], float(EXPERTS), 128.0, ALU.add, ALU.mult)
            dve.drain()
            v.tensor_scalar(index_all[:, 0:SEQS, 3].rearrange("p (g s) -> p g s", s=GROUP),
                            route_f[:, :].unsqueeze(2).broadcast_to([128, ROUTES, GROUP]),
                            C[:, C_PART:C_PART + 1], None, ALU.add)
            dve.wait_ge(hashT_ready, 1)
            v.tensor_copy(index_all[:, 0:SEQS, 0:3], front_a[:, 0:384].rearrange("p (n s) -> p s n", n=3))
            dve.drain()
            v.tensor_copy(index_cur[:, :], index_all[:, 0, :]).then_inc(cur_ready, 1)
            dve.wait_ge(experts_loaded, 64)
            for l in range(2):
                v.tensor_tensor(ws_sb[:, l, :], ws_sb[:, l, :], ident, ALU.add)
            dve.drain()
            for l in range(2):
                cols = slice(l * HID, (l + 1) * HID)
                v.tensor_tensor(experts[:, 0:EXPERTS, cols], wr_sb[:, l, :, :],
                                ws_sb[:, l, :].unsqueeze(1).broadcast_to([HID, EXPERTS, HID]), ALU.add)
                v.tensor_copy(experts[:, EXPERTS, cols], ws_sb[:, l, :])
                v.tensor_scalar(experts[:, 0:EXPERTS, 2 * HID + l], br_sb[:, l, :], bs_sb[:, l:l + 1], None, ALU.add)
                v.tensor_copy(experts[:, EXPERTS, 2 * HID + l:2 * HID + l + 1], bs_sb[:, l:l + 1])
            dve.drain().then_inc(experts_ready, 1)

            front(0)
            for h in range(HEADS):
                select(0, h)
            carry()
            with dve.Fori(0, SEQS - 1) as i:
                front(i + 1)
                for h in range(HEADS):
                    back(i, h)
                    if h == HEADS - 1:
                        finish(i)
                    select(i + 1, h)
                wait(dve, out_stored, 16 * i + 16)
                carry()
            for h in range(HEADS):
                back(SEQS - 1, h)
            finish(SEQS - 1)

        @block.tensor
        def _(pe):
            mm = nc.tensor.matmul

            def transpose_norm(s, n, src):
                wait(pe, xn_ready, s * LAYER_NORMS + n + 1)
                nc.tensor.transpose(front_a[0:DIM, 0:TOK], src, ident).then_inc(xnT_ps_ready, 1)
                wait(pe, xnT_ready, s * LAYER_NORMS + n + 1)

            def front(s):
                transpose_norm(s, 0, xn[:, :])
                mm(front_b[0:DIM, 0:128], attn_w_sb[:, 0, :], xnT[:, :], start=True, stop=True)
                mm(front_b[0:DIM, 128:256], attn_w_sb[:, 1, :], xnT[:, :], start=True, stop=True)
                mm(front_b[:, 256:256 + DIM], xnT[:, :], attn_w_sb[:, 2, :], start=True, stop=True).then_inc(qkv_ps_ready, 1)
                wait(pe, qkv_ready, s + 1)
                mm(front_a[:, 128:256], qkT[:, 0, :], qkT[:, 1, :], start=True, stop=True).then_inc(scores_ready, 1)
                wait(pe, probs_ready, s + 1)
                nc.tensor.transpose(front_a[:, 256:384], probs[:, :], ident).then_inc(pT_ps_ready, 1)
                wait(pe, pT_ready, s + 1)
                mm(front_b[:, 384:384 + DIM], probsT[:, :], v0[:, :], start=True, stop=True).then_inc(attn_ps_ready, 1)
                transpose_norm(s, 1, xn[:, :])
                mm(front_b[:, 0:128], wi_sb[:, :], xnT[:, :], start=True, stop=True).then_inc(hid_ps_ready, 1)
                for n in range(2):
                    wait(pe, hid_ready, 3 * s + n + 1)
                    mm(front_b[:, 128 * (n + 1):128 * (n + 2)], expert_w[:, n * HID:(n + 1) * HID], hidT[:, n, :],
                       start=True, stop=True).then_inc(hid_ps_ready, 1)
                wait(pe, hid_ready, 3 * s + 3)
                mm(front_a[:, 384:384 + DIM], hidT[:, 2, :], wo_ffn_sb[:, :], start=True, stop=False)
                mm(front_a[:, 384:384 + DIM], ones_row[:, :], bo_sb[:, :], start=False, stop=True).then_inc(ffn_ps_ready, 1)
                transpose_norm(s, 2, x2[:, :])
                mm(front_b[:, 0:128], xnT[:, :], qkv_sb[:, DIM:3 * DIM], start=True, stop=True)
                mm(front_b[0:DIM, 128:256], qkv_sb[:, 0:DIM], xnT[:, :], start=True, stop=True).then_inc(qkv1_ps_ready, 1)
                wait(pe, qkv1_ready, s + 1)
                mm(front_a[0:DIM, 128:128 + DIM], kv1[:, 0:DIM], kv1[:, DIM:2 * DIM], start=True, stop=False)
                mm(front_a[0:DIM, 128:128 + DIM], ident[0:DIM, 0:DIM], block_mask, start=False, stop=True).then_inc(mix_ps_ready, 1)
                wait(pe, mixn_ready, s + 1)
                nc.tensor.transpose(front_a[0:DIM, 256:256 + DIM], mixn[:, :], ident[0:DIM, 0:DIM]).then_inc(mixT_ps_ready, 1)
                wait(pe, mixT_ready, s + 1)
                mm(front_a[:, 384:384 + DIM], q1T[:, :], mixT[:, :], start=True, stop=True).then_inc(xf_ps_ready, 1)
                transpose_norm(s, 3, xn[:, :])
                mm(front_b[0:MLP_HALF, 0:128], fc1_sb[:, 0:MLP_HALF], xnT[:, :], start=True, stop=True)
                mm(front_b[0:MLP_HALF, 128:256], fc1_sb[:, MLP_HALF:MLP], xnT[:, :], start=True, stop=True).then_inc(fc1_ps_ready, 1)
                wait(pe, gelu_ready, s + 1)
                mm(front_b[:, 384:384 + DIM], geluT[:, 0, :], fc2_sb[:, 0, :], start=True, stop=False)
                mm(front_b[:, 384:384 + DIM], geluT[:, 1, :], fc2_sb[:, 1, :], start=False, stop=False)
                mm(front_b[:, 384:384 + DIM], ones_row[:, :], bfc2_sb[:, :], start=False, stop=True).then_inc(mlp_ps_ready, 1)
                transpose_norm(s, 4, xn[:, :])
                for c in range(4):
                    last = mm(front_b[:, 128 * c:128 * c + 128], wq_pk_sb[:, 128 * c:128 * c + 128], xnT[0:DIM, :], start=True, stop=True)
                last.then_inc(qpk_ps_ready, 1)
                wait(pe, qpk_ready, s + 1)
                for b in range(2):
                    for c in range(2):
                        last = mm(sim_ps[b][:, 256 * c:256 * c + 256], qpkT[:, 2 * b + c, :],
                                  keys_sb[:, 2 * b + c, :, :].rearrange("p a k -> p (a k)"), start=True, stop=True)
                    last.then_inc(sim_ps_ready, 1)

            def back(s, h):
                n = s * HEADS + h
                if h == 0:
                    wait(pe, carried, s + 1)
                wait(pe, diag_ready, n + 1)
                wait(pe, rows_loaded[h], 16 * TOP * s + 16 * TOP)
                mm(kv_ps[0:DIM, 128:256], wq_sb[:, h * DIM:(h + 1) * DIM], x4T_cur[:, :], start=True, stop=True)
                for k in range(TOP):
                    last = mm(kv_ps[:, 0:TOK], rows[:, h, k, :], diag[:, h % 2, k, :], start=(k == 0), stop=(k == TOP - 1))
                last.then_inc(kv_done, 1)
                wait(pe, kvT_ready, n + 1)
                nc.tensor.transpose(turn_ps[:, 0:DIM], kvT[DIM:2 * DIM, :], ident[DIM:2 * DIM, DIM:2 * DIM]).then_inc(v_ready, 1)
                mm(score_ps[:, 0:TOK], qhT[:, :], kvT[0:DIM, :], start=True, stop=False)
                mm(score_ps[:, 0:TOK], ident, causal, start=False, stop=True).then_inc(b_scores_ready, 1)
                wait(pe, b_norm_ready, n + 1)
                nc.tensor.transpose(turn_ps[:, 128:256], b_norm[:, :], ident).then_inc(b_pT_ps_ready, 1)
                wait(pe, b_pT_ready, n + 1)
                wait(pe, b_probs_ready, n + 1)
                mm(turn_ps[0:DIM, 256:384], v_rows[:, :], b_probsT[:, :], start=True, stop=True).then_inc(headT_ps_ready, 1)
                wait(pe, headT_ready, n + 1)
                last = mm(y_ps[:, 0:DIM], headT[:, :], wo_sb[:, h, :], start=(h == 0), stop=(h == HEADS - 1))
                if h == HEADS - 1:
                    last.then_inc(y_ready, 1)

            pe.wait_ge(const_loaded, 16)
            pe.wait_ge(hashed, 1)
            for n in range(3):
                last = nc.tensor.transpose(front_a[:, 128 * n:128 * n + 128], hashes[:, n, :], ident)
            last.then_inc(hashT_ready, 1)
            pe.wait_ge(loaded, N_LOADED)
            pe.wait_ge(consts_set, 1)
            front(0)
            with pe.Fori(0, SEQS - 1) as i:
                front(i + 1)
                for h in range(HEADS):
                    back(i, h)
            for h in range(HEADS):
                back(SEQS - 1, h)


def kernel(**inputs):
    import concourse.bacc as _bacc
    from concourse.bass_utils import run_bass_kernel_spmd as _run

    a = {k: np.ascontiguousarray(v) for k, v in inputs.items()}

    def aug(w, b):
        return np.concatenate([w, b[None, :]], axis=0)

    arrays = {
        "x": a["x"], "emb2": a["L0_tok_emb_2"], "emb3": a["L0_tok_emb_3"], "emb4": a["L0_tok_emb_4"],
        "attn_w": np.stack([aug(a[f"L0_attn_W{c}"].T, a[f"L0_attn_b{c}"]) for c in "qkv"], axis=1),
        "wi_aug": aug(a["L0_ffn_Wi"].T, a["L0_ffn_bi"]),
        "route": a["L0_ffn_route_id"],
        "wr": a["L0_ffn_Wr"].transpose(3, 0, 1, 2), "br": a["L0_ffn_br"].transpose(2, 0, 1),
        "ws": a["L0_ffn_Ws"][:, 0].transpose(2, 0, 1), "bs": a["L0_ffn_bs"][:, 0].T,
        "wo_ffn": a["L0_ffn_Wo"].T, "bo": a["L0_ffn_bo"][None, :],
        "qkv_aug": aug(a["L1_attn_w_qkv"], a["L1_attn_b_qkv"]),
        "norm_gb": np.stack([a["L1_attn_norm_g"], a["L1_attn_norm_b"]], axis=1),
        "fc1_aug": aug(a["L1_attn_w_fc1"], a["L1_attn_b_fc1"]),
        "fc2": a["L1_attn_w_fc2"].reshape(2, MLP_HALF, DIM).transpose(1, 0, 2), "bfc2": a["L1_attn_b_fc2"][None, :],
        "wq_pk": a["L1_ffn_Wq_pk"], "pk_keys": a["L1_ffn_pk_keys"].transpose(0, 2, 3, 1), "wq": a["L1_ffn_Wq"],
        "kv_table": np.concatenate([a["L1_ffn_keys_table"], a["L1_ffn_values_table"]], axis=1),
        "wo": a["L1_ffn_Wo"].reshape(HEADS, DIM, DIM).transpose(1, 0, 2),
        "const": constants(),
    }
    arrays = {f"in_{k}": np.ascontiguousarray(v) for k, v in arrays.items()}
    nc = _bacc.Bacc("TRN2", target_bir_lowering=False, num_devices=1)
    args = [nc.dram_tensor(k, v.shape, mybir.dt.from_np(v.dtype), kind="ExternalInput").ap() for k, v in arrays.items()]
    args.append(nc.dram_tensor("out", (SEQS, TOK, DIM), F32, kind="ExternalOutput").ap())
    tower(nc, *args)
    r = _run(nc, [arrays], core_ids=[0])
    return r.results[0]["out"]
```

```python
import numpy as np
import concourse.bass as bass
from concourse import mybir
from contextlib import ExitStack

ACT = mybir.ActivationFunctionType
ALU = mybir.AluOpType
AX = mybir.AxisListType
F32 = mybir.dt.float32
I32 = mybir.dt.int32
U32 = mybir.dt.uint32

SEQS, TOK, DIM = 128, 128, 64
GRAMS = (2, 3, 4)
PRIME, VOCAB = 31, 125000
HID, EXPERTS, GROUP = 128, 16, 2
ROUTES = SEQS // GROUP
EXPERT_ROW = 2 * HID + 2
HEAD_DIM = 16
MLP, MLP_HALF = 192, 96
HEADS, KEYS, KEY_DIM, TOP = 8, 64, 32, 16
EPS = 1e-5
MASKED = -1e30
REPLACED = -3.0e38
STAIRS = [(0, 1, 16), (1, 1, 8), (2, 1, 5), (3, 1, 4), (4, 1, 3), (5, 3, 2), (8, 8, 1)]
PAIRS = sum(n * m for _, n, m in STAIRS)
STEPS = 4
FRONT_STEPS = HEADS * STEPS
INDEX_COLS = 4

C_ID, C_CAUSAL, C_BLOCK, C_IOTA, C_GRAM, C_PART, C_EPS = 0, 128, 256, 320, 320 + PAIRS, 323 + PAIRS, 324 + PAIRS
C_COLS = 325 + PAIRS


def constants():
    c = np.zeros((128, C_COLS), np.float32)
    c[:, C_ID:C_ID + 128] = np.eye(128)
    c[:, C_CAUSAL:C_CAUSAL + 128] = np.triu(np.full((128, 128), MASKED), 1)
    head = np.arange(DIM) // HEAD_DIM
    c[:DIM, C_BLOCK:C_BLOCK + DIM] = np.where(head[:, None] == head[None, :], 0.0, MASKED)
    c[:, C_IOTA:C_IOTA + PAIRS] = np.arange(PAIRS)
    for n, g in enumerate(GRAMS):
        c[g - 1:, C_GRAM + n] = 1.0 / (len(GRAMS) + 1)
    c[:, C_PART] = np.arange(128)
    c[:, C_EPS] = EPS
    return c


def tower(nc, x, emb2, emb3, emb4, attn_w, wi_aug, route, wr, br, ws, bs, wo_ffn, bo, qkv_aug, norm_gb,
          fc1_aug, fc2, bfc2, wq_pk, pk_keys, wq, kv_table, wo, const, out):
    ctx = ExitStack()
    with ctx:
        def sb(name, shape, dt=F32):
            return ctx.enter_context(nc.sbuf_tensor(name, shape, dt))

        def pb(name):
            return ctx.enter_context(nc.psum_tensor(name, [128, 512], F32))

        def sem(name):
            return ctx.enter_context(nc.semaphore(name))

        expert_table = nc.dram_tensor("expert_table", ((EXPERTS + 1) * 128, EXPERT_ROW), F32).ap()

        C = sb("C", [128, C_COLS])
        ident = C[:, C_ID:C_ID + 128]
        causal = C[:, C_CAUSAL:C_CAUSAL + 128]
        block_mask = C[0:DIM, C_BLOCK:C_BLOCK + DIM]
        iota = C[:, C_IOTA:C_IOTA + PAIRS]
        eps = C[:, C_EPS:C_EPS + 1]
        attn_w_sb = sb("attn_w_sb", [DIM + 1, 3, DIM])
        wi_sb = sb("wi_sb", [DIM + 1, HID])
        wo_ffn_sb = sb("wo_ffn_sb", [HID, DIM])
        bo_sb = sb("bo_sb", [1, DIM])
        qkv_sb = sb("qkv_sb", [DIM + 1, 3 * DIM])
        gb_sb = sb("gb_sb", [DIM, 2])
        fc1_sb = sb("fc1_sb", [DIM + 1, MLP])
        fc2_sb = sb("fc2_sb", [MLP_HALF, 2, DIM])
        bfc2_sb = sb("bfc2_sb", [1, DIM])
        wq_pk_sb = sb("wq_pk_sb", [DIM, 2 * HEADS * KEY_DIM])
        keys_sb = sb("keys_sb", [128, 4, 4, KEYS])
        wq_sb = sb("wq_sb", [DIM, HEADS * DIM])
        wo_sb = sb("wo_sb", [DIM, HEADS, DIM])
        ones_row = sb("ones_row", [1, 128])

        ids = sb("ids", [SEQS, TOK], I32)
        idf = sb("idf", [SEQS, TOK])
        hashes = sb("hashes", [SEQS, 3, TOK])
        quot_i = sb("quot_i", [SEQS, 3, TOK], I32)
        quot = sb("quot", [SEQS, 3, TOK])
        index_all = sb("index_all", [TOK, SEQS + 3, INDEX_COLS], I32)
        route_i = sb("route_i", [128, ROUTES], I32)
        route_f = sb("route_f", [128, ROUTES])
        route_ok = sb("route_ok", [128, ROUTES])
        wr_sb = sb("wr_sb", [HID, 2, EXPERTS, HID])
        br_sb = sb("br_sb", [HID, 2, EXPERTS])
        ws_sb = sb("ws_sb", [HID, 2, HID])
        bs_sb = sb("bs_sb", [HID, 2])
        experts = sb("experts", [HID, EXPERTS + 1, EXPERT_ROW])

        index_cur = sb("index_cur", [TOK, INDEX_COLS], I32)
        emb = sb("emb", [TOK, 3, DIM])
        expert_w = sb("expert_w", [HID, EXPERT_ROW])
        stats = sb("stats", [TOK, 6])
        mv = sb("mv", [TOK, 2])
        std = sb("std", [TOK, 1])
        rstd = sb("rstd", [TOK, 1])
        h0 = sb("h0", [TOK, DIM])
        h1 = sb("h1", [TOK, DIM])
        h2 = sb("h2", [TOK, DIM])
        h3 = sb("h3", [TOK, DIM])
        xn = sb("xn", [TOK, DIM])
        xnT = sb("xnT", [DIM + 1, TOK])
        x2 = sb("x2", [TOK, DIM])
        x3 = sb("x3", [TOK, DIM])
        mlp_sum = sb("mlp_sum", [TOK, DIM])
        qkT = sb("qkT", [DIM, 2, TOK])
        v0 = sb("v0", [TOK, DIM])
        rowmax = sb("rowmax", [TOK, 1])
        negmax = sb("negmax", [TOK, 1])
        probs = sb("probs", [TOK, TOK])
        rowsum = sb("rowsum", [TOK, 1])
        rsum = sb("rsum", [TOK, 1])
        probsT = sb("probsT", [TOK, TOK])
        hidT = sb("hidT", [HID, 3, TOK])
        kv1 = sb("kv1", [TOK, 2 * DIM])
        q1T = sb("q1T", [DIM, TOK])
        mix = sb("mix", [DIM, DIM])
        mixn = sb("mixn", [DIM, DIM])
        mixT = sb("mixT", [DIM, DIM])
        geluT = sb("geluT", [MLP_HALF, 2, TOK])
        qpkT = sb("qpkT", [128, 4, TOK])
        sims = sb("sims", [TOK, 2 * HEADS, KEYS])

        top = sb("top", [TOK, 2, 2, TOP])
        pos = sb("pos", [TOK, 2, TOP], U32)
        rest = sb("rest", [TOK, 2, KEYS])
        pairs = sb("pairs", [TOK, 2, PAIRS])
        pairs_rest = sb("pairs_rest", [TOK, PAIRS])
        best = sb("best", [TOK, TOP])
        best_pos = sb("best_pos", [TOK, TOP], U32)
        onehot = sb("onehot", [TOK, TOP, PAIRS])
        negbest = sb("negbest", [TOK, 1])
        expbest = sb("expbest", [TOK, TOP])
        expsum = sb("expsum", [TOK, 1])
        rexp = sb("rexp", [TOK, 1])
        weight = sb("weight", [TOK, HEADS, TOP])
        row_index = sb("row_index", [TOK, HEADS, TOP], I32)

        rows = sb("rows", [TOK, HEADS, TOP, 2 * DIM])
        diag = sb("diag", [TOK, 2, TOP, TOK])
        h3_next = sb("h3_next", [TOK, DIM])
        x4T_next = sb("x4T_next", [DIM, TOK])
        h3_cur = sb("h3_cur", [TOK, DIM])
        x4T_cur = sb("x4T_cur", [DIM, TOK])
        x4T = xnT[0:DIM, :]
        qhT = sb("qhT", [DIM, TOK])
        kvT = sb("kvT", [2 * DIM, TOK])
        v_rows = sb("v_rows", [TOK, DIM])
        b_max = sb("b_max", [TOK, 1])
        b_neg = sb("b_neg", [TOK, 1])
        b_probs = sb("b_probs", [TOK, TOK])
        b_sum = sb("b_sum", [TOK, 1])
        b_rsum = sb("b_rsum", [TOK, 1])
        b_norm = sb("b_norm", [TOK, TOK])
        b_probsT = sb("b_probsT", [TOK, TOK])
        headT = sb("headT", [DIM, TOK])
        out_sb = sb("out_sb", [TOK, DIM])

        front_a, front_b = pb("front_a"), pb("front_b")
        sim_ps = [pb("sim_ps0"), pb("sim_ps1")]
        kv_ps = pb("kv_ps")
        score_ps = pb("score_ps")
        turn_ps = pb("turn_ps")
        y_ps = pb("y_ps")

        loaded = sem("loaded")
        ids_loaded = sem("ids_loaded")
        experts_loaded = sem("experts_loaded")
        const_loaded = sem("const_loaded")
        consts_set = sem("consts_set")
        keys_cleared = sem("keys_cleared")
        hashed = sem("hashed")
        hashT_ready = sem("hashT_ready")
        experts_ready = sem("experts_ready")
        experts_stored = sem("experts_stored")
        cur_ready = sem("cur_ready")
        emb_loaded = sem("emb_loaded")
        expert_arrived = sem("expert_arrived")
        emb_used = sem("emb_used")
        held = sem("held")
        var_ready, std_ready = sem("var_ready"), sem("std_ready")
        xn_ready, xnT_ps_ready, xnT_ready = sem("xn_ready"), sem("xnT_ps_ready"), sem("xnT_ready")
        qkv_ps_ready, qkv_ready = sem("qkv_ps_ready"), sem("qkv_ready")
        scores_ready, negmax_ready, probs_ready = sem("scores_ready"), sem("negmax_ready"), sem("probs_ready")
        pT_ps_ready, pT_ready, attn_ps_ready = sem("pT_ps_ready"), sem("pT_ready"), sem("attn_ps_ready")
        hid_ps_ready, hid_ready, ffn_ps_ready = sem("hid_ps_ready"), sem("hid_ready"), sem("ffn_ps_ready")
        qkv1_ps_ready, qkv1_ready = sem("qkv1_ps_ready"), sem("qkv1_ready")
        mix_ps_ready, mixmax_ready, mix_ready = sem("mix_ps_ready"), sem("mixmax_ready"), sem("mix_ready")
        mixn_ready, mixT_ps_ready, mixT_ready = sem("mixn_ready"), sem("mixT_ps_ready"), sem("mixT_ready")
        xf_ps_ready = sem("xf_ps_ready")
        fc1_ps_ready, gelu_ready, mlp_ps_ready = sem("fc1_ps_ready"), sem("gelu_ready"), sem("mlp_ps_ready")
        qpk_ps_ready, qpk_ready = sem("qpk_ps_ready"), sem("qpk_ready")
        sim_ps_ready, sims_ready = sem("sim_ps_ready"), sem("sims_ready")
        best_ready, expbest_ready = sem("best_ready"), sem("expbest_ready")
        weight_ready, index_ready = sem("weight_ready"), sem("index_ready")
        rows_loaded = [sem(f"rows_loaded{h}") for h in range(HEADS)]
        diag_ready, kv_done, qhT_ready = sem("diag_ready"), sem("kv_done"), sem("qhT_ready")
        kvT_ready, b_scores_ready, v_ready = sem("kvT_ready"), sem("b_scores_ready"), sem("v_ready")
        b_neg_ready, b_probs_ready, b_norm_ready = sem("b_neg_ready"), sem("b_probs_ready"), sem("b_norm_ready")
        b_pT_ps_ready, b_pT_ready = sem("b_pT_ps_ready"), sem("b_pT_ready")
        headT_ps_ready, headT_ready, y_ready = sem("headT_ps_ready"), sem("headT_ready"), sem("y_ready")
        q_ps_ready, sims_used, x4T_used = sem("q_ps_ready"), sem("sims_used"), sem("x4T_used")
        carried, out_ready, out_stored = sem("carried"), sem("out_ready"), sem("out_stored")

        def wait(eng, semaphore, count):
            eng.wait_ge(semaphore, count)
            if not isinstance(count, int):
                eng.sem_inc(held, 1)

        LAYER_NORMS = 5
        SMALL_LOADS = [(attn_w_sb, attn_w), (wi_sb, wi_aug), (wo_ffn_sb, wo_ffn), (bo_sb, bo), (qkv_sb, qkv_aug),
                       (gb_sb, norm_gb), (fc1_sb, fc1_aug), (fc2_sb, fc2), (bfc2_sb, bfc2), (wq_pk_sb, wq_pk),
                       (wq_sb, wq), (wo_sb, wo)]
        N_LOADED = 16 * (len(SMALL_LOADS) + 2 * HEADS)

        block = ctx.enter_context(nc.Block())

        @block.sync
        def _(sp):
            sp.dma_start(C[:, :], const).then_inc(const_loaded, 16)
            sp.dma_start(ids[:, :], x).then_inc(ids_loaded, 16)
            sp.dma_start(route_i[:, :], route.partition_broadcast(128)).then_inc(ids_loaded, 16)
            for dst, src in ((wr_sb, wr), (br_sb, br), (ws_sb, ws), (bs_sb, bs)):
                sp.dma_start(dst[:], src).then_inc(experts_loaded, 16)
            for dst, src in SMALL_LOADS:
                sp.dma_start(dst[:], src).then_inc(loaded, 16)
            sp.wait_ge(keys_cleared, 1)
            for half in range(2):
                for h in range(HEADS):
                    q = h % 4
                    sp.dma_start(keys_sb[q * KEY_DIM:(q + 1) * KEY_DIM, half * 2 + h // 4, q, :],
                                 pk_keys[half, h, :, :]).then_inc(loaded, 16)
            sp.wait_ge(experts_ready, 1)
            sp.dma_start(expert_table.rearrange("(e p) c -> p e c", p=128), experts[:]).then_inc(experts_stored, 16)

            def store(s):
                wait(sp, out_ready, s + 1)
                sp.dma_start(out[bass.ds(s, 1), :, :].rearrange("a t d -> t (a d)"), out_sb[:, :]).then_inc(out_stored, 16)

            with sp.Fori(0, SEQS) as s:
                store(s)
            sp.wait_ge(out_stored, 16 * SEQS)
            sp.wait_ge(experts_stored, 16)

        @block.gpsimd
        def _(pool):
            def gather(dst, table, index):
                return nc.gpsimd.indirect_dma_start(out=dst, out_offset=None, in_=table,
                                                    in_offset=bass.IndirectOffsetOnAxis(ap=index, axis=0))

            def token_rows(s, first=False):
                wait(pool, cur_ready, s + 1)
                if not first:
                    wait(pool, emb_used, s)
                    wait(pool, ffn_ps_ready, s)
                for n, table in enumerate((emb2, emb3, emb4)):
                    gather(emb[:, n, :], table, index_cur[:, n:n + 1]).then_inc(emb_loaded, 16)
                gather(expert_w[:, :], expert_table, index_cur[:, 3:4]).then_inc(expert_arrived, 16)

            def head_rows(s, h):
                wait(pool, index_ready, s * HEADS + h + 1)
                for k in range(TOP):
                    gather(rows[:, h, k, :], kv_table, row_index[:, h, k:k + 1]).then_inc(rows_loaded[h], 16)

            pool.wait_ge(experts_stored, 16)
            token_rows(0, first=True)
            token_rows(1)
            for h in range(HEADS):
                head_rows(0, h)
            token_rows(2)
            with pool.Fori(0, SEQS - 2) as i:
                for h in range(HEADS):
                    wait(pool, kv_done, i * HEADS + h + 1)
                    head_rows(i + 1, h)
                    if h == HEADS // 2 - 1:
                        token_rows(i + 3)
            for h in range(HEADS):
                wait(pool, kv_done, (SEQS - 2) * HEADS + h + 1)
                head_rows(SEQS - 1, h)
            pool.wait_ge(emb_loaded, 48 * (SEQS + 1))
            pool.wait_ge(expert_arrived, 16 * (SEQS + 1))


        @block.scalar
        def _(act):
            def copy(dst, src):
                return nc.scalar.activation(dst, src, ACT.Copy)

            def layer_std(s, n):
                wait(act, var_ready, s * LAYER_NORMS + n + 1)
                nc.scalar.activation(std[:, :], mv[:, 1:2], ACT.Sqrt, bias=eps).then_inc(std_ready, 1)

            def transposed(s, n):
                wait(act, xnT_ps_ready, s * LAYER_NORMS + n + 1)
                copy(xnT[0:DIM, :], front_a[0:DIM, 0:TOK]).then_inc(xnT_ready, 1)

            def front(s, step):
                if step == 0:
                    layer_std(s, 0)
                elif step == 1:
                    transposed(s, 0)
                elif step == 2:
                    wait(act, qkv_ps_ready, s + 1)
                    copy(qkT[:, :, :], front_b[0:DIM, 0:2 * TOK].rearrange("p (a t) -> p a t", a=2))
                    copy(v0[:, :], front_b[:, 256:256 + DIM]).then_inc(qkv_ready, 1)
                elif step == 4:
                    wait(act, negmax_ready, s + 1)
                    nc.scalar.activation(probs[:, :], front_a[:, 128:256], ACT.Exp, bias=negmax[:, :],
                                         scale=DIM ** -0.5, accum_out=rowsum[:, :]).then_inc(probs_ready, 1)
                elif step == 5:
                    wait(act, pT_ps_ready, s + 1)
                    copy(probsT[:, :], front_a[:, 256:384]).then_inc(pT_ready, 1)
                elif step == 7:
                    layer_std(s, 1)
                elif step == 8:
                    transposed(s, 1)
                elif step in (9, 10, 11):
                    n = step - 9
                    wait(act, hid_ps_ready, 3 * s + n + 1)
                    bias = {} if n == 0 else {"bias": expert_w[:, 2 * HID + n - 1:2 * HID + n]}
                    nc.scalar.activation(hidT[:, n, :], front_b[:, 128 * n:128 * n + 128], ACT.Relu, **bias).then_inc(hid_ready, 1)
                elif step == 13:
                    layer_std(s, 2)
                elif step == 14:
                    transposed(s, 2)
                elif step == 15:
                    wait(act, qkv1_ps_ready, s + 1)
                    copy(kv1[:, :], front_b[:, 0:128])
                    copy(q1T[:, :], front_b[0:DIM, 128:256]).then_inc(qkv1_ready, 1)
                elif step == 17:
                    wait(act, mixmax_ready, s + 1)
                    nc.scalar.activation(mix[:, :], front_a[0:DIM, 128:128 + DIM], ACT.Exp, bias=negmax[0:DIM, :],
                                         scale=HEAD_DIM ** -0.5, accum_out=rowsum[0:DIM, :]).then_inc(mix_ready, 1)
                elif step == 18:
                    wait(act, mixT_ps_ready, s + 1)
                    copy(mixT[:, :], front_a[0:DIM, 256:256 + DIM]).then_inc(mixT_ready, 1)
                elif step == 20:
                    layer_std(s, 3)
                elif step == 21:
                    wait(act, xnT_ps_ready, s * LAYER_NORMS + 4)
                    nc.scalar.activation(xnT[0:DIM, :], front_a[0:DIM, 0:TOK], ACT.Identity, bias=gb_sb[:, 1:2],
                                         scale=gb_sb[:, 0:1]).then_inc(xnT_ready, 1)
                elif step == 22:
                    wait(act, fc1_ps_ready, s + 1)
                    nc.scalar.activation(geluT[:, :, :], front_b[0:MLP_HALF, 0:256].rearrange("p (a t) -> p a t", a=2),
                                         ACT.Gelu).then_inc(gelu_ready, 1)
                elif step == 24:
                    layer_std(s, 4)
                elif step == 25:
                    transposed(s, 4)
                elif step == 26:
                    wait(act, qpk_ps_ready, s + 1)
                    copy(qpkT[:, :, :], front_b[:, :].rearrange("p (a t) -> p a t", a=4)).then_inc(qpk_ready, 1)
                elif step == 30:
                    if not isinstance(s, int) or s > 0:
                        wait(act, sims_used, s)
                    for b in range(2):
                        wait(act, sim_ps_ready, 2 * s + b + 1)
                        copy(sims[:, 8 * b:8 * b + 8, :], sim_ps[b][:, :].rearrange("p (a t) -> p a t", a=8)).then_inc(sims_ready, 1)

            def select(s, h, step):
                if step == 1:
                    wait(act, best_ready, s * HEADS + h + 1)
                    nc.scalar.activation(expbest[:, :], best[:, :], ACT.Exp, bias=negbest[:, :],
                                         accum_out=expsum[:, :]).then_inc(expbest_ready, 1)

            def diagonals(s, h, step, steps=STEPS):
                if step == 0:
                    wait(act, weight_ready, s * HEADS + h + 1)
                for k in range(TOP // steps * step, TOP // steps * (step + 1)):
                    last = nc.scalar.activation(diag[:, h % 2, k, :], ident, ACT.Copy, scale=weight[:, h, k:k + 1])
                if step == steps - 1:
                    last.then_inc(diag_ready, 1)

            def back(s, h, step, last_seq=False):
                n = s * HEADS + h
                if step == 0:
                    wait(act, kv_done, n + 1)
                    copy(kvT[:, :], kv_ps[:, 128 * (h % 2):128 * (h % 2) + TOK])
                    wait(act, q_ps_ready, n + 1)
                    copy(qhT[:, :], turn_ps[0:DIM, 384:512]).then_inc(kvT_ready, 1)
                elif step == 1:
                    wait(act, v_ready, n + 1)
                    copy(v_rows[:, :], turn_ps[:, 0:DIM])
                    wait(act, b_neg_ready, n + 1)
                    nc.scalar.activation(b_probs[:, :], score_ps[:, 0:TOK], ACT.Exp, bias=b_neg[:, :],
                                         scale=DIM ** -0.5, accum_out=b_sum[:, :]).then_inc(b_probs_ready, 1)
                if h + 2 < HEADS:
                    diagonals(s, h + 2, step)
                elif not last_seq:
                    diagonals(s + 1, h + 2 - HEADS, step)

            act.wait_ge(const_loaded, 16)
            act.wait_ge(loaded, N_LOADED)
            for step in range(FRONT_STEPS):
                front(0, step)
            for h in range(HEADS):
                for step in range(STEPS):
                    front(1, h * STEPS + step)
                    select(0, h, step)
            for h in range(2):
                diagonals(0, h, 0, steps=1)
            with act.Fori(0, SEQS - 2) as i:
                for h in range(HEADS):
                    for step in range(STEPS):
                        front(i + 2, h * STEPS + step)
                        select(i + 1, h, step)
                        back(i, h, step)
            for h in range(HEADS):
                for step in range(STEPS):
                    select(SEQS - 1, h, step)
                    back(SEQS - 2, h, step)
            for h in range(HEADS):
                for step in range(STEPS):
                    back(SEQS - 1, h, step, last_seq=True)

        @block.vector
        def _(dve):
            v = nc.vector

            def moments(src):
                dve.drain()
                v.bn_stats(stats[:, :], src)
                dve.drain()
                v.bn_aggr(mv[:, :], stats[:, :]).then_inc(var_ready, 1)

            def normalize(s, n, src, dst):
                wait(dve, std_ready, s * LAYER_NORMS + n + 1)
                v.reciprocal(rstd[:, :], std[:, :])
                dve.drain()
                v.tensor_scalar(dst, src, mv[:, 0:1], rstd[:, :], ALU.subtract, ALU.mult).then_inc(xn_ready, 1)

            def negated_max(scores, high, low, scale):
                v.reduce_max(high, scores, AX.X)
                dve.drain()
                return v.tensor_scalar(low, high, -scale, None, ALU.mult)

            def front(s, step):
                if step == 0:
                    wait(dve, emb_loaded, 48 * s + 48)
                    wait(dve, expert_arrived, 16 * s + 16)
                    v.tensor_copy(index_cur[:, :], index_all[:, bass.ds(s + 1, 1), :].rearrange("p a c -> p (a c)")).then_inc(cur_ready, 1)
                    v.tensor_scalar(h0[:, :], emb[:, 0, :], C[:, C_GRAM:C_GRAM + 1], None, ALU.mult)
                    dve.drain()
                    v.scalar_tensor_tensor(h0[:, :], emb[:, 1, :], C[:, C_GRAM + 1:C_GRAM + 2], h0[:, :], ALU.mult, ALU.add)
                    dve.drain()
                    v.scalar_tensor_tensor(h0[:, :], emb[:, 2, :], C[:, C_GRAM + 2:C_GRAM + 3], h0[:, :], ALU.mult, ALU.add).then_inc(emb_used, 1)
                    moments(h0[:, :])
                elif step == 1:
                    normalize(s, 0, h0[:, :], xn[:, :])
                elif step == 4:
                    wait(dve, scores_ready, s + 1)
                    negated_max(front_a[:, 128:256], rowmax[:, :], negmax[:, :], DIM ** -0.5).then_inc(negmax_ready, 1)
                elif step == 7:
                    wait(dve, probs_ready, s + 1)
                    v.reciprocal(rsum[:, :], rowsum[:, :])
                    dve.drain()
                    wait(dve, attn_ps_ready, s + 1)
                    v.scalar_tensor_tensor(h1[:, :], front_b[:, 384:384 + DIM], rsum[:, :], h0[:, :], ALU.mult, ALU.add)
                    moments(h1[:, :])
                elif step == 8:
                    normalize(s, 1, h1[:, :], xn[:, :])
                elif step == 13:
                    wait(dve, ffn_ps_ready, s + 1)
                    v.tensor_tensor(h2[:, :], h1[:, :], front_a[:, 384:384 + DIM], ALU.add)
                    moments(h2[:, :])
                elif step == 14:
                    normalize(s, 2, h2[:, :], x2[:, :])
                elif step == 17:
                    wait(dve, mix_ps_ready, s + 1)
                    negated_max(front_a[0:DIM, 128:128 + DIM], rowmax[0:DIM, :], negmax[0:DIM, :], HEAD_DIM ** -0.5).then_inc(mixmax_ready, 1)
                elif step == 18:
                    wait(dve, mix_ready, s + 1)
                    v.reciprocal(rsum[0:DIM, :], rowsum[0:DIM, :])
                    dve.drain()
                    v.tensor_scalar(mixn[:, :], mix[:, :], rsum[0:DIM, :], None, ALU.mult).then_inc(mixn_ready, 1)
                elif step == 20:
                    wait(dve, xf_ps_ready, s + 1)
                    v.tensor_tensor(x3[:, :], x2[:, :], front_a[:, 384:384 + DIM], ALU.add)
                    moments(x3[:, :])
                elif step == 21:
                    normalize(s, 3, x3[:, :], xn[:, :])
                elif step == 24:
                    wait(dve, mlp_ps_ready, s + 1)
                    v.tensor_tensor(mlp_sum[:, :], x3[:, :], front_b[:, 384:384 + DIM], ALU.add)
                    dve.drain()
                    v.tensor_tensor(h3[:, :], h2[:, :], mlp_sum[:, :], ALU.add)
                    moments(h3[:, :])
                elif step == 25:
                    normalize(s, 4, h3[:, :], xn[:, :])

            def select(s, h, step):
                n = s * HEADS + h
                part = [sims[:, h, :], sims[:, HEADS + h, :]]
                if step == 0:
                    if h == 0:
                        wait(dve, sims_ready, 2 * s + 2)
                    for a in range(2):
                        v.max(top[:, a, 0, 0:8], part[a])
                    dve.drain()
                    for a in range(2):
                        v.max_index(pos[:, a, 0:8], top[:, a, 0, 0:8], part[a])
                    for a in range(2):
                        last = v.match_replace(rest[:, a, :], top[:, a, 0, 0:8], part[a], REPLACED)
                    if h == HEADS - 1:
                        last.then_inc(sims_used, 1)
                    dve.drain()
                    for a in range(2):
                        v.max(top[:, a, 0, 8:16], rest[:, a, :])
                    dve.drain()
                    for a in range(2):
                        v.max_index(pos[:, a, 8:16], top[:, a, 0, 8:16], rest[:, a, :])
                elif step == 1:
                    dve.drain()
                    v.tensor_scalar(top[:, 0, 1, :], pos[:, 0, :], float(h * KEYS * KEYS), None, ALU.add)
                    v.tensor_scalar(top[:, 1, 1, :], pos[:, 1, :], float(KEYS), None, ALU.mult)
                    dve.drain()
                    at = 0
                    for i0, ni, nj in STAIRS:
                        v.tensor_tensor(pairs[:, :, at:at + ni * nj].rearrange("p a (i j) -> p a i j", i=ni),
                                        top[:, 0, :, i0:i0 + ni].unsqueeze(3).broadcast_to([TOK, 2, ni, nj]),
                                        top[:, 1, :, 0:nj].unsqueeze(2).broadcast_to([TOK, 2, ni, nj]), ALU.add)
                        at += ni * nj
                    dve.drain()
                    v.max(best[:, 0:8], pairs[:, 0, :])
                    dve.drain()
                    v.tensor_scalar(negbest[:, :], best[:, 0:1], -1.0, None, ALU.mult)
                    v.max_index(best_pos[:, 0:8], best[:, 0:8], pairs[:, 0, :])
                    v.match_replace(pairs_rest[:, :], best[:, 0:8], pairs[:, 0, :], REPLACED)
                    dve.drain()
                    v.max(best[:, 8:16], pairs_rest[:, :]).then_inc(best_ready, 1)
                elif step == 2:
                    dve.drain()
                    v.max_index(best_pos[:, 8:16], best[:, 8:16], pairs_rest[:, :])
                    dve.drain()
                    v.tensor_tensor(onehot[:, :, :], best_pos[:, :].unsqueeze(2).broadcast_to([TOK, TOP, PAIRS]),
                                    iota.unsqueeze(1).broadcast_to([TOK, TOP, PAIRS]), ALU.is_equal)
                    dve.drain()
                    v.tensor_tensor(onehot[:, :, :], onehot[:, :, :], pairs[:, 1, :].unsqueeze(1).broadcast_to([TOK, TOP, PAIRS]), ALU.mult)
                elif step == 3:
                    dve.drain()
                    with nc.allow_low_precision(reason="one row number and zeros: exact"):
                        v.tensor_reduce(row_index[:, h, :], onehot[:, :, :], AX.X, ALU.add).then_inc(index_ready, 1)
                    wait(dve, expbest_ready, n + 1)
                    v.reciprocal(rexp[:, :], expsum[:, :])
                    dve.drain()
                    v.tensor_scalar(weight[:, h, :], expbest[:, :], rexp[:, :], None, ALU.mult).then_inc(weight_ready, 1)

            def back(s, h, step):
                n = s * HEADS + h
                if step == 1:
                    wait(dve, b_scores_ready, n + 1)
                    negated_max(score_ps[:, 0:TOK], b_max[:, :], b_neg[:, :], DIM ** -0.5).then_inc(b_neg_ready, 1)
                elif step == 2:
                    wait(dve, b_probs_ready, n + 1)
                    v.reciprocal(b_rsum[:, :], b_sum[:, :])
                    dve.drain()
                    v.tensor_scalar(b_norm[:, :], b_probs[:, :], b_rsum[:, :], None, ALU.mult).then_inc(b_norm_ready, 1)
                elif step == 3:
                    wait(dve, b_pT_ps_ready, n + 1)
                    v.tensor_copy(b_probsT[:, :], turn_ps[:, 128:256]).then_inc(b_pT_ready, 1)

            def back_end(s, h):
                wait(dve, headT_ps_ready, s * HEADS + h + 1)
                v.tensor_copy(headT[:, :], turn_ps[0:DIM, 256:384]).then_inc(headT_ready, 1)

            def finish(s):
                wait(dve, y_ready, s + 1)
                v.tensor_tensor(out_sb[:, :], h3_cur[:, :], y_ps[:, 0:DIM], ALU.add).then_inc(out_ready, 1)

            def carry(first=False):
                if not first:
                    v.tensor_copy(h3_cur[:, :], h3_next[:, :])
                    v.tensor_copy(x4T_cur[:, :], x4T_next[:, :]).then_inc(carried, 1)
                    dve.drain()
                v.tensor_copy(h3_next[:, :], h3[:, :])
                v.tensor_copy(x4T_next[:, :], x4T).then_inc(x4T_used, 1)

            v.memset(keys_sb[:], 0.0).then_inc(keys_cleared, 1)
            v.memset(ones_row[:, :], 1.0)
            v.memset(xnT[DIM:DIM + 1, :], 1.0).then_inc(consts_set, 1)
            v.memset(hashes[:], 0.0)
            v.memset(index_all[:], 0)
            dve.wait_ge(ids_loaded, 32)
            v.tensor_copy(idf[:, :], ids[:, :])
            v.tensor_copy(route_f[:, :], route_i[:, :])
            dve.drain()
            for n, g in enumerate(GRAMS):
                back_by = g - 1
                newer = idf[:, back_by:] if n == 0 else hashes[:, n - 1, back_by:]
                v.scalar_tensor_tensor(hashes[:, n, back_by:], idf[:, 0:TOK - back_by], float(PRIME ** back_by % VOCAB),
                                       newer, ALU.mult, ALU.add)
                dve.drain()
            v.tensor_scalar(quot_i[:], hashes[:], 1.0 / VOCAB, None, ALU.mult)
            dve.drain()
            v.tensor_copy(quot[:], quot_i[:])
            dve.drain()
            v.scalar_tensor_tensor(hashes[:], quot[:], float(-VOCAB), hashes[:], ALU.mult, ALU.add)
            dve.drain()
            v.tensor_scalar(quot[:], hashes[:], 0.0, float(VOCAB), ALU.is_lt, ALU.mult)
            dve.drain()
            v.tensor_tensor(hashes[:], hashes[:], quot[:], ALU.add)
            dve.drain()
            v.tensor_scalar(quot[:], hashes[:], float(VOCAB), float(-VOCAB), ALU.is_ge, ALU.mult)
            dve.drain()
            v.tensor_tensor(hashes[:], hashes[:], quot[:], ALU.add).then_inc(hashed, 1)
            dve.wait_ge(const_loaded, 16)
            v.tensor_scalar(route_ok[:, :], route_f[:, :], 0.0, None, ALU.is_ge)
            dve.drain()
            v.scalar_tensor_tensor(route_ok[:, :], route_f[:, :], float(EXPERTS - 1), route_ok[:, :], ALU.is_le, ALU.mult)
            dve.drain()
            v.scalar_tensor_tensor(route_f[:, :], route_f[:, :], float(-EXPERTS), route_ok[:, :], ALU.add, ALU.mult)
            dve.drain()
            v.tensor_scalar(route_f[:, :], route_f[:, :], float(EXPERTS), 128.0, ALU.add, ALU.mult)
            dve.drain()
            v.tensor_scalar(index_all[:, 0:SEQS, 3].rearrange("p (g s) -> p g s", s=GROUP),
                            route_f[:, :].unsqueeze(2).broadcast_to([128, ROUTES, GROUP]),
                            C[:, C_PART:C_PART + 1], None, ALU.add)
            dve.wait_ge(hashT_ready, 1)
            v.tensor_copy(index_all[:, 0:SEQS, 0:3], front_a[:, 0:384].rearrange("p (n s) -> p s n", n=3))
            dve.drain()
            v.tensor_copy(index_cur[:, :], index_all[:, 0, :]).then_inc(cur_ready, 1)
            dve.wait_ge(experts_loaded, 64)
            for l in range(2):
                v.tensor_tensor(ws_sb[:, l, :], ws_sb[:, l, :], ident, ALU.add)
            dve.drain()
            for l in range(2):
                cols = slice(l * HID, (l + 1) * HID)
                v.tensor_tensor(experts[:, 0:EXPERTS, cols], wr_sb[:, l, :, :],
                                ws_sb[:, l, :].unsqueeze(1).broadcast_to([HID, EXPERTS, HID]), ALU.add)
                v.tensor_copy(experts[:, EXPERTS, cols], ws_sb[:, l, :])
                v.tensor_scalar(experts[:, 0:EXPERTS, 2 * HID + l], br_sb[:, l, :], bs_sb[:, l:l + 1], None, ALU.add)
                v.tensor_copy(experts[:, EXPERTS, 2 * HID + l:2 * HID + l + 1], bs_sb[:, l:l + 1])
            dve.drain().then_inc(experts_ready, 1)

            for step in range(FRONT_STEPS):
                front(0, step)
            dve.wait_ge(qpk_ps_ready, 1)
            carry(first=True)
            for h in range(HEADS):
                for step in range(STEPS):
                    front(1, h * STEPS + step)
                    select(0, h, step)
            dve.wait_ge(qpk_ps_ready, 2)
            carry()
            with dve.Fori(0, SEQS - 2) as i:
                for h in range(HEADS):
                    for step in range(STEPS):
                        front(i + 2, h * STEPS + step)
                        back(i, h, step)
                        select(i + 1, h, step)
                    back_end(i, h)
                finish(i)
                wait(dve, qpk_ps_ready, i + 3)
                wait(dve, out_stored, 16 * i + 16)
                carry()
            for h in range(HEADS):
                for step in range(STEPS):
                    back(SEQS - 2, h, step)
                    select(SEQS - 1, h, step)
                back_end(SEQS - 2, h)
            finish(SEQS - 2)
            dve.wait_ge(out_stored, 16 * (SEQS - 1))
            carry()
            for h in range(HEADS):
                for step in range(STEPS):
                    back(SEQS - 1, h, step)
                back_end(SEQS - 1, h)
            finish(SEQS - 1)

        @block.tensor
        def _(pe):
            mm = nc.tensor.matmul

            def transpose_norm(s, n, src):
                wait(pe, xn_ready, s * LAYER_NORMS + n + 1)
                nc.tensor.transpose(front_a[0:DIM, 0:TOK], src, ident).then_inc(xnT_ps_ready, 1)

            def front(s, step):
                if step == 1:
                    if not isinstance(s, int) or s > 0:
                        wait(pe, x4T_used, s)
                    transpose_norm(s, 0, xn[:, :])
                elif step == 2:
                    wait(pe, xnT_ready, s * LAYER_NORMS + 1)
                    mm(front_b[0:DIM, 0:128], attn_w_sb[:, 0, :], xnT[:, :], start=True, stop=True)
                    mm(front_b[0:DIM, 128:256], attn_w_sb[:, 1, :], xnT[:, :], start=True, stop=True)
                    mm(front_b[:, 256:256 + DIM], xnT[:, :], attn_w_sb[:, 2, :], start=True, stop=True).then_inc(qkv_ps_ready, 1)
                elif step == 3:
                    wait(pe, qkv_ready, s + 1)
                    mm(front_a[:, 128:256], qkT[:, 0, :], qkT[:, 1, :], start=True, stop=True).then_inc(scores_ready, 1)
                elif step == 5:
                    wait(pe, probs_ready, s + 1)
                    nc.tensor.transpose(front_a[:, 256:384], probs[:, :], ident).then_inc(pT_ps_ready, 1)
                elif step == 6:
                    wait(pe, pT_ready, s + 1)
                    mm(front_b[:, 384:384 + DIM], probsT[:, :], v0[:, :], start=True, stop=True).then_inc(attn_ps_ready, 1)
                elif step == 8:
                    transpose_norm(s, 1, xn[:, :])
                elif step == 9:
                    wait(pe, xnT_ready, s * LAYER_NORMS + 2)
                    mm(front_b[:, 0:128], wi_sb[:, :], xnT[:, :], start=True, stop=True).then_inc(hid_ps_ready, 1)
                elif step in (10, 11):
                    n = step - 10
                    wait(pe, hid_ready, 3 * s + n + 1)
                    mm(front_b[:, 128 * (n + 1):128 * (n + 2)], expert_w[:, n * HID:(n + 1) * HID], hidT[:, n, :],
                       start=True, stop=True).then_inc(hid_ps_ready, 1)
                elif step == 12:
                    wait(pe, hid_ready, 3 * s + 3)
                    mm(front_a[:, 384:384 + DIM], hidT[:, 2, :], wo_ffn_sb[:, :], start=True, stop=False)
                    mm(front_a[:, 384:384 + DIM], ones_row[:, :], bo_sb[:, :], start=False, stop=True).then_inc(ffn_ps_ready, 1)
                elif step == 14:
                    transpose_norm(s, 2, x2[:, :])
                elif step == 15:
                    wait(pe, xnT_ready, s * LAYER_NORMS + 3)
                    mm(front_b[:, 0:128], xnT[:, :], qkv_sb[:, DIM:3 * DIM], start=True, stop=True)
                    mm(front_b[0:DIM, 128:256], qkv_sb[:, 0:DIM], xnT[:, :], start=True, stop=True).then_inc(qkv1_ps_ready, 1)
                elif step == 16:
                    wait(pe, qkv1_ready, s + 1)
                    mm(front_a[0:DIM, 128:128 + DIM], kv1[:, 0:DIM], kv1[:, DIM:2 * DIM], start=True, stop=False)
                    mm(front_a[0:DIM, 128:128 + DIM], ident[0:DIM, 0:DIM], block_mask, start=False, stop=True).then_inc(mix_ps_ready, 1)
                elif step == 18:
                    wait(pe, mixn_ready, s + 1)
                    nc.tensor.transpose(front_a[0:DIM, 256:256 + DIM], mixn[:, :], ident[0:DIM, 0:DIM]).then_inc(mixT_ps_ready, 1)
                elif step == 19:
                    wait(pe, mixT_ready, s + 1)
                    mm(front_a[:, 384:384 + DIM], q1T[:, :], mixT[:, :], start=True, stop=True).then_inc(xf_ps_ready, 1)
                elif step == 21:
                    transpose_norm(s, 3, xn[:, :])
                elif step == 22:
                    wait(pe, xnT_ready, s * LAYER_NORMS + 4)
                    mm(front_b[0:MLP_HALF, 0:128], fc1_sb[:, 0:MLP_HALF], xnT[:, :], start=True, stop=True)
                    mm(front_b[0:MLP_HALF, 128:256], fc1_sb[:, MLP_HALF:MLP], xnT[:, :], start=True, stop=True).then_inc(fc1_ps_ready, 1)
                elif step == 23:
                    wait(pe, gelu_ready, s + 1)
                    mm(front_b[:, 384:384 + DIM], geluT[:, 0, :], fc2_sb[:, 0, :], start=True, stop=False)
                    mm(front_b[:, 384:384 + DIM], geluT[:, 1, :], fc2_sb[:, 1, :], start=False, stop=False)
                    mm(front_b[:, 384:384 + DIM], ones_row[:, :], bfc2_sb[:, :], start=False, stop=True).then_inc(mlp_ps_ready, 1)
                elif step == 25:
                    transpose_norm(s, 4, xn[:, :])
                elif step == 26:
                    wait(pe, xnT_ready, s * LAYER_NORMS + 5)
                    for c in range(4):
                        last = mm(front_b[:, 128 * c:128 * c + 128], wq_pk_sb[:, 128 * c:128 * c + 128], xnT[0:DIM, :], start=True, stop=True)
                    last.then_inc(qpk_ps_ready, 1)
                elif step == 27:
                    wait(pe, qpk_ready, s + 1)
                    for b in range(2):
                        for c in range(2):
                            last = mm(sim_ps[b][:, 256 * c:256 * c + 256], qpkT[:, 2 * b + c, :],
                                      keys_sb[:, 2 * b + c, :, :].rearrange("p a k -> p (a k)"), start=True, stop=True)
                        last.then_inc(sim_ps_ready, 1)

            def weighted_sum(s, h, first, count):
                n = s * HEADS + h
                if first == 0:
                    wait(pe, diag_ready, n + 1)
                    wait(pe, rows_loaded[h], 16 * TOP * s + 16 * TOP)
                for k in range(first, first + count):
                    last = mm(kv_ps[:, 128 * (h % 2):128 * (h % 2) + TOK], rows[:, h, k, :], diag[:, h % 2, k, :],
                              start=(k == 0), stop=(k == TOP - 1))
                if first + count == TOP:
                    last.then_inc(kv_done, 1)

            def back(s, h, step, last_seq=False):
                n = s * HEADS + h
                if step == 0:
                    if h == 0:
                        wait(pe, carried, s + 1)
                    mm(turn_ps[0:DIM, 384:512], wq_sb[:, h * DIM:(h + 1) * DIM], x4T_cur[:, :], start=True, stop=True).then_inc(q_ps_ready, 1)
                    wait(pe, kvT_ready, n + 1)
                    nc.tensor.transpose(turn_ps[:, 0:DIM], kvT[DIM:2 * DIM, :], ident[DIM:2 * DIM, DIM:2 * DIM]).then_inc(v_ready, 1)
                    mm(score_ps[:, 0:TOK], qhT[:, :], kvT[0:DIM, :], start=True, stop=False)
                    mm(score_ps[:, 0:TOK], ident, causal, start=False, stop=True).then_inc(b_scores_ready, 1)
                elif step == 2:
                    wait(pe, b_norm_ready, n + 1)
                    nc.tensor.transpose(turn_ps[:, 128:256], b_norm[:, :], ident).then_inc(b_pT_ps_ready, 1)
                elif step == 3:
                    wait(pe, b_pT_ready, n + 1)
                    mm(turn_ps[0:DIM, 256:384], v_rows[:, :], b_probsT[:, :], start=True, stop=True).then_inc(headT_ps_ready, 1)
                if step in (1, 2):
                    half = (step - 1) * TOP // 2
                    if h + 1 < HEADS:
                        weighted_sum(s, h + 1, half, TOP // 2)
                    elif not last_seq:
                        weighted_sum(s + 1, 0, half, TOP // 2)

            def back_end(s, h):
                wait(pe, headT_ready, s * HEADS + h + 1)
                last = mm(y_ps[:, 0:DIM], headT[:, :], wo_sb[:, h, :], start=(h == 0), stop=(h == HEADS - 1))
                if h == HEADS - 1:
                    last.then_inc(y_ready, 1)

            pe.wait_ge(const_loaded, 16)
            pe.wait_ge(hashed, 1)
            for n in range(3):
                last = nc.tensor.transpose(front_a[:, 128 * n:128 * n + 128], hashes[:, n, :], ident)
            last.then_inc(hashT_ready, 1)
            pe.wait_ge(loaded, N_LOADED)
            pe.wait_ge(consts_set, 1)
            for s in range(2):
                for step in range(FRONT_STEPS):
                    front(s, step)
            weighted_sum(0, 0, 0, TOP)
            with pe.Fori(0, SEQS - 2) as i:
                for h in range(HEADS):
                    for step in range(STEPS):
                        front(i + 2, h * STEPS + step)
                        back(i, h, step)
                    back_end(i, h)
            for h in range(HEADS):
                for step in range(STEPS):
                    back(SEQS - 2, h, step)
                back_end(SEQS - 2, h)
            for h in range(HEADS):
                for step in range(STEPS):
                    back(SEQS - 1, h, step, last_seq=True)
                back_end(SEQS - 1, h)


def kernel(**inputs):
    import concourse.bacc as _bacc
    from concourse.bass_utils import run_bass_kernel_spmd as _run

    a = {k: np.ascontiguousarray(v) for k, v in inputs.items()}

    def aug(w, b):
        return np.concatenate([w, b[None, :]], axis=0)

    arrays = {
        "x": a["x"], "emb2": a["L0_tok_emb_2"], "emb3": a["L0_tok_emb_3"], "emb4": a["L0_tok_emb_4"],
        "attn_w": np.stack([aug(a[f"L0_attn_W{c}"].T, a[f"L0_attn_b{c}"]) for c in "qkv"], axis=1),
        "wi_aug": aug(a["L0_ffn_Wi"].T, a["L0_ffn_bi"]),
        "route": a["L0_ffn_route_id"],
        "wr": a["L0_ffn_Wr"].transpose(3, 0, 1, 2), "br": a["L0_ffn_br"].transpose(2, 0, 1),
        "ws": a["L0_ffn_Ws"][:, 0].transpose(2, 0, 1), "bs": a["L0_ffn_bs"][:, 0].T,
        "wo_ffn": a["L0_ffn_Wo"].T, "bo": a["L0_ffn_bo"][None, :],
        "qkv_aug": aug(a["L1_attn_w_qkv"], a["L1_attn_b_qkv"]),
        "norm_gb": np.stack([a["L1_attn_norm_g"], a["L1_attn_norm_b"]], axis=1),
        "fc1_aug": aug(a["L1_attn_w_fc1"], a["L1_attn_b_fc1"]),
        "fc2": a["L1_attn_w_fc2"].reshape(2, MLP_HALF, DIM).transpose(1, 0, 2), "bfc2": a["L1_attn_b_fc2"][None, :],
        "wq_pk": a["L1_ffn_Wq_pk"], "pk_keys": a["L1_ffn_pk_keys"].transpose(0, 2, 3, 1), "wq": a["L1_ffn_Wq"],
        "kv_table": np.concatenate([a["L1_ffn_keys_table"], a["L1_ffn_values_table"]], axis=1),
        "wo": a["L1_ffn_Wo"].reshape(HEADS, DIM, DIM).transpose(1, 0, 2),
        "const": constants(),
    }
    arrays = {f"in_{k}": np.ascontiguousarray(v) for k, v in arrays.items()}
    nc = _bacc.Bacc("TRN2", target_bir_lowering=False, num_devices=1)
    args = [nc.dram_tensor(k, v.shape, mybir.dt.from_np(v.dtype), kind="ExternalInput").ap() for k, v in arrays.items()]
    args.append(nc.dram_tensor("out", (SEQS, TOK, DIM), F32, kind="ExternalOutput").ap())
    tower(nc, *args)
    r = _run(nc, [arrays], core_ids=[0])
    return r.results[0]["out"]
```

```python
import numpy as np
import concourse.bass as bass
from concourse import mybir
from contextlib import ExitStack

ACT = mybir.ActivationFunctionType
ALU = mybir.AluOpType
AX = mybir.AxisListType
F32 = mybir.dt.float32
I32 = mybir.dt.int32
BF16 = mybir.dt.bfloat16
U32 = mybir.dt.uint32

SEQS, TOK, DIM = 128, 128, 64
GRAMS = (2, 3, 4)
PRIME, VOCAB = 31, 125000
HID, EXPERTS, GROUP = 128, 16, 2
ROUTES = SEQS // GROUP
EXPERT_ROW = 2 * HID + 2
HEAD_DIM = 16
MLP, MLP_HALF = 192, 96
HEADS, KEYS, KEY_DIM, TOP = 8, 64, 32, 16
EPS = 1e-5
MASKED = -1e30
REPLACED = -3.0e38
STAIRS = [(0, 1, 16), (1, 1, 8), (2, 1, 5), (3, 1, 4), (4, 1, 3), (5, 3, 2), (8, 8, 1)]
PAIRS = sum(n * m for _, n, m in STAIRS)
STEPS = 4
FRONT_STEPS = HEADS * STEPS
INDEX_COLS = 4

GATHERED = 6
DENSE = HEADS - GATHERED
SLOTS = KEYS * KEYS // 128
GROUP_SLOTS = 2
GROUP_COLS = GROUP_SLOTS * TOK
GROUPS = SLOTS // GROUP_SLOTS
NOT_RANKED = 64
HEAD_A, HEAD_B = GATHERED, GATHERED + 1
UNITS = [HEAD_B, 0, 1, 2, 3, HEAD_A, 4, 5]
SUMS_AT = {0: 0, 1: 1, 2: 2, 3: 3, 4: 4, 6: 5}
DIAGONALS_AT = {0: 1, 1: 2, 2: 3, 3: 4, 5: 5, 7: 0}

C_ID, C_CAUSAL, C_BLOCK, C_IOTA, C_GRAM, C_PART, C_EPS = 0, 128, 256, 320, 320 + PAIRS, 323 + PAIRS, 324 + PAIRS
C_COLS = 326 + PAIRS


def constants():
    c = np.zeros((128, C_COLS), np.float32)
    c[:, C_ID:C_ID + 128] = np.eye(128)
    c[:, C_CAUSAL:C_CAUSAL + 128] = np.triu(np.full((128, 128), MASKED), 1)
    head = np.arange(DIM) // HEAD_DIM
    c[:DIM, C_BLOCK:C_BLOCK + DIM] = np.where(head[:, None] == head[None, :], 0.0, MASKED)
    c[:, C_IOTA:C_IOTA + PAIRS] = np.arange(PAIRS)
    for n, g in enumerate(GRAMS):
        c[g - 1:, C_GRAM + n] = 1.0 / (len(GRAMS) + 1)
    c[:, C_PART] = np.arange(128)
    c[:, C_EPS] = EPS
    c[:, C_EPS + 1] = 1.5
    return c


def selections():
    pair = np.arange(KEYS * KEYS)
    m = np.zeros((2 * KEYS, KEYS * KEYS), np.float32)
    m[pair % KEYS, pair] = 1.0
    m[KEYS + pair // KEYS, pair] = 1.0
    return m


def key_numbers():
    return np.tile(np.repeat(np.arange(KEYS, dtype=np.float32), TOP), (128, 1))


def tower(nc, x, emb2, emb3, emb4, attn_w, wi_aug, route, wr, br, ws, bs, wo_ffn, bo, qkv_aug, norm_gb,
          fc1_aug, fc2, bfc2, wq_pk, pk_keys, wq, kv_table, wo, const, sel, key_no, out):
    ctx = ExitStack()
    with ctx:
        def sb(name, shape, dt=F32):
            return ctx.enter_context(nc.sbuf_tensor(name, shape, dt))

        def pb(name):
            return ctx.enter_context(nc.psum_tensor(name, [128, 512], F32))

        def sem(name):
            return ctx.enter_context(nc.semaphore(name))

        expert_table = nc.dram_tensor("expert_table", ((EXPERTS + 1) * 128, EXPERT_ROW), F32).ap()

        C = sb("C", [128, C_COLS])
        ident = C[:, C_ID:C_ID + 128]
        causal = C[:, C_CAUSAL:C_CAUSAL + 128]
        block_mask = C[0:DIM, C_BLOCK:C_BLOCK + DIM]
        iota = C[:, C_IOTA:C_IOTA + PAIRS]
        eps = C[:, C_EPS:C_EPS + 1]
        one_and_half = C[:, C_EPS + 1:C_EPS + 2]
        attn_w_sb = sb("attn_w_sb", [DIM + 1, 3, DIM])
        wi_sb = sb("wi_sb", [DIM + 1, HID])
        wo_ffn_sb = sb("wo_ffn_sb", [HID, DIM])
        bo_sb = sb("bo_sb", [1, DIM])
        qkv_sb = sb("qkv_sb", [DIM + 1, 3 * DIM])
        gb_sb = sb("gb_sb", [DIM, 2])
        fc1_sb = sb("fc1_sb", [DIM + 1, MLP])
        fc2_sb = sb("fc2_sb", [MLP_HALF, 2, DIM])
        bfc2_sb = sb("bfc2_sb", [1, DIM])
        wq_pk_sb = sb("wq_pk_sb", [DIM, 2 * HEADS * KEY_DIM])
        keys_sb = sb("keys_sb", [128, 4, 4, KEYS])
        wq_sb = sb("wq_sb", [DIM, HEADS * DIM])
        wo_sb = sb("wo_sb", [DIM, HEADS, DIM])
        ones_row = sb("ones_row", [1, 128])

        ids = sb("ids", [SEQS, TOK], I32)
        idf = sb("idf", [SEQS, TOK])
        hashes = sb("hashes", [SEQS, 3, TOK])
        quot_i = sb("quot_i", [SEQS, 3, TOK], I32)
        quot = sb("quot", [SEQS, 3, TOK])
        index_all = sb("index_all", [TOK, SEQS + 3, INDEX_COLS], I32)
        route_i = sb("route_i", [128, ROUTES], I32)
        route_f = sb("route_f", [128, ROUTES])
        route_ok = sb("route_ok", [128, ROUTES])
        rows = sb("rows", [TOK, GATHERED, TOP, 2 * DIM])
        space = rows[:, :, :, :].rearrange("p h k d -> p (h k d)")
        wr_sb = space[:, 0:2 * EXPERTS * HID].rearrange("p (l e c) -> p l e c", l=2, e=EXPERTS)
        experts = space[:, 2 * EXPERTS * HID:2 * EXPERTS * HID + (EXPERTS + 1) * EXPERT_ROW].rearrange("p (e c) -> p e c", e=EXPERTS + 1)
        br_sb = sb("br_sb", [HID, 2, EXPERTS])
        ws_sb = sb("ws_sb", [HID, 2, HID])
        bs_sb = sb("bs_sb", [HID, 2])

        index_cur = sb("index_cur", [TOK, INDEX_COLS], I32)
        emb = sb("emb", [TOK, 3, DIM])
        expert_w = sb("expert_w", [HID, EXPERT_ROW])
        stats = sb("stats", [TOK, 6])
        mv = sb("mv", [TOK, 2])
        var_eps, lnvar, root, root_v, neg_half, factor = (
            sb(name, [TOK, 1]) for name in ("var_eps", "lnvar", "root", "root_v", "neg_half", "factor"))
        rstd = sb("rstd", [TOK, 1])
        h0 = sb("h0", [TOK, DIM])
        h1 = sb("h1", [TOK, DIM])
        h2 = sb("h2", [TOK, DIM])
        h3 = sb("h3", [TOK, DIM])
        xn = sb("xn", [TOK, DIM])
        xnT = sb("xnT", [DIM + 1, TOK])
        x2 = sb("x2", [TOK, DIM])
        x3 = sb("x3", [TOK, DIM])
        mlp_sum = sb("mlp_sum", [TOK, DIM])
        qkT = sb("qkT", [DIM, 2, TOK])
        v0 = sb("v0", [TOK, DIM])
        rowmax = sb("rowmax", [TOK, 1])
        negmax = sb("negmax", [TOK, 1])
        probs = sb("probs", [TOK, TOK])
        rowsum = sb("rowsum", [TOK, 1])
        rsum = sb("rsum", [TOK, 1])
        probsT = sb("probsT", [TOK, TOK])
        hidT = sb("hidT", [HID, 3, TOK])
        kv1 = sb("kv1", [TOK, 2 * DIM])
        q1T = sb("q1T", [DIM, TOK])
        mix = sb("mix", [DIM, DIM])
        mixn = sb("mixn", [DIM, DIM])
        mixT = sb("mixT", [DIM, DIM])
        geluT = sb("geluT", [MLP_HALF, 2, TOK])
        qpkT = sb("qpkT", [128, 4, TOK])
        sims = sb("sims", [TOK, 2 * HEADS, KEYS])

        top = sb("top", [TOK, 2, 2, TOP])
        pos = sb("pos", [TOK, 2, TOP], U32)
        rest = sb("rest", [TOK, 2, KEYS])
        pairs = sb("pairs", [TOK, 2, PAIRS])
        pairs_rest = sb("pairs_rest", [TOK, PAIRS])
        best = sb("best", [TOK, TOP])
        best_pos = sb("best_pos", [TOK, TOP], U32)
        onehot = sb("onehot", [TOK, TOP, PAIRS])
        negbest = sb("negbest", [TOK, 1])
        expbest = sb("expbest", [TOK, TOP])
        expsum = sb("expsum", [TOK, 1])
        rexp = sb("rexp", [TOK, 1])
        weight = sb("weight", [TOK, GATHERED, TOP])
        row_index = sb("row_index", [TOK, GATHERED, TOP], I32)

        table = sb("table", [128, DENSE, SLOTS, 2 * DIM])
        sel_sb = sb("sel_sb", [2 * KEYS, SLOTS, 128])
        sel_bf = sb("sel_bf", [2 * KEYS, SLOTS, 128], BF16)
        key_no_f = sb("key_no_f", [TOK, KEYS, TOP])
        key_no_bf = sb("key_no_bf", [TOK, KEYS, TOP], BF16)
        pos_bf = sb("pos_bf", [TOK, 2, TOP], BF16)
        rank_code = sb("rank_code", [TOK, 2, TOP], BF16)
        selected = sb("selected", [TOK, PAIRS])
        key_hot = sb("key_hot", [TOK, 2, KEYS, TOP], BF16)
        key_code = sb("key_code", [TOK, 2, KEYS])
        lnsum = sb("lnsum", [TOK, 1])
        shift = sb("shift", [TOK, 1])
        key_score = sb("key_score", [TOK, 2, KEYS])
        scoreT = sb("scoreT", [2 * KEYS, DENSE, TOK])
        codeT = sb("codeT", [2 * KEYS, DENSE, TOK], BF16)
        pair_exp = sb("pair_exp", [128, 2, GROUP_COLS])
        pair_weight = sb("pair_weight", [128, 2, GROUP_COLS])

        diag = sb("diag", [TOK, 2, TOP, TOK])
        h3_next = sb("h3_next", [TOK, DIM])
        x4T_next = sb("x4T_next", [DIM, TOK])
        h3_cur = sb("h3_cur", [TOK, DIM])
        x4T_cur = sb("x4T_cur", [DIM, TOK])
        x4T = xnT[0:DIM, :]
        qhT = [sb(f"qhT{p}", [DIM, TOK]) for p in range(2)]
        kvT = [sb(f"kvT{p}", [2 * DIM, TOK]) for p in range(2)]
        v_rows = [sb(f"v_rows{p}", [TOK, DIM]) for p in range(2)]
        b_max = [sb(f"b_max{p}", [TOK, 1]) for p in range(2)]
        b_neg = [sb(f"b_neg{p}", [TOK, 1]) for p in range(2)]
        b_probs = [sb(f"b_probs{p}", [TOK, TOK]) for p in range(2)]
        b_sum = [sb(f"b_sum{p}", [TOK, 1]) for p in range(2)]
        b_rsum = [sb(f"b_rsum{p}", [TOK, 1]) for p in range(2)]
        b_norm = [sb(f"b_norm{p}", [TOK, TOK]) for p in range(2)]
        b_probsT = [sb(f"b_probsT{p}", [TOK, TOK]) for p in range(2)]
        headT = [sb(f"headT{p}", [DIM, TOK]) for p in range(2)]
        y_sum = sb("y_sum", [TOK, DIM])
        out_sb = sb("out_sb", [TOK, DIM])

        front_a, front_b = pb("front_a"), pb("front_b")
        kv_ps = pb("kv_ps")
        dense_ps = pb("dense_ps")
        turn_ps = [pb("turn_ps0"), pb("turn_ps1")]
        pair_ps = [pb("pair_ps0"), pb("pair_ps1")]
        score_ps = [b[:, 128:256] for b in turn_ps]
        y_ps = [b[:, 0:DIM] for b in turn_ps]
        sim_ps = front_b
        code_ps = {HEAD_B: front_b, HEAD_A: front_a}

        loaded = sem("loaded")
        ids_loaded = sem("ids_loaded")
        experts_loaded = sem("experts_loaded")
        const_loaded = sem("const_loaded")
        consts_set = sem("consts_set")
        keys_cleared = sem("keys_cleared")
        hashed = sem("hashed")
        hashT_ready = sem("hashT_ready")
        experts_ready = sem("experts_ready")
        experts_stored = sem("experts_stored")
        cur_ready = sem("cur_ready")
        emb_loaded = sem("emb_loaded")
        expert_arrived = sem("expert_arrived")
        emb_used = sem("emb_used")
        held = sem("held")
        var_ready, rstd_ready = sem("var_ready"), sem("rstd_ready")
        xn_ready, xnT_ps_ready, xnT_ready = sem("xn_ready"), sem("xnT_ps_ready"), sem("xnT_ready")
        qkv_ps_ready, qkv_ready = sem("qkv_ps_ready"), sem("qkv_ready")
        scores_ready, negmax_ready, probs_ready = sem("scores_ready"), sem("negmax_ready"), sem("probs_ready")
        pT_ps_ready, pT_ready, attn_ps_ready = sem("pT_ps_ready"), sem("pT_ready"), sem("attn_ps_ready")
        hid_ps_ready, hid_ready, ffn_ps_ready = sem("hid_ps_ready"), sem("hid_ready"), sem("ffn_ps_ready")
        qkv1_ps_ready, qkv1_ready = sem("qkv1_ps_ready"), sem("qkv1_ready")
        mix_ps_ready, mixmax_ready, mix_ready = sem("mix_ps_ready"), sem("mixmax_ready"), sem("mix_ready")
        mixn_ready, mixT_ps_ready, mixT_ready = sem("mixn_ready"), sem("mixT_ps_ready"), sem("mixT_ready")
        xf_ps_ready = sem("xf_ps_ready")
        fc1_ps_ready, gelu_ready, mlp_ps_ready = sem("fc1_ps_ready"), sem("gelu_ready"), sem("mlp_ps_ready")
        qpk_ps_ready, qpk_ready = sem("qpk_ps_ready"), sem("qpk_ready")
        sim_ps_ready, sims_ready = sem("sim_ps_ready"), sem("sims_ready")
        best_ready, expbest_ready = sem("best_ready"), sem("expbest_ready")
        weight_ready, index_ready = sem("weight_ready"), sem("index_ready")
        rows_loaded = [sem(f"rows_loaded{h}") for h in range(GATHERED)]
        diag_ready, kv_done = sem("diag_ready"), sem("kv_done")
        kvT_ready, v_ready, v_copied, y_added = sem("kvT_ready"), sem("v_ready"), sem("v_copied"), sem("y_added")
        b_neg_ready, b_probs_ready, b_norm_ready = sem("b_neg_ready"), sem("b_probs_ready"), sem("b_norm_ready")
        b_pT_ps_ready, b_pT_ready = sem("b_pT_ps_ready"), sem("b_pT_ready")
        headT_ps_ready, headT_ready = sem("headT_ps_ready"), sem("headT_ready")
        q_ps_ready, sims_used, x4T_used = sem("q_ps_ready"), sem("sims_used"), sem("x4T_used")
        score_code_ready, code_ps_ready, codeT_ready = sem("score_code_ready"), sem("code_ps_ready"), sem("codeT_ready")
        pair_ps_ready, pair_exp_ready, pair_weight_ready = sem("pair_ps_ready"), sem("pair_exp_ready"), sem("pair_weight_ready")
        dense_done, dense_set = [sem("dense_done_a"), sem("dense_done_b")], sem("dense_set")
        tables_loaded, y_ps_ready = sem("tables_loaded"), sem("y_ps_ready")
        carried, out_ready, out_stored = sem("carried"), sem("out_ready"), sem("out_stored")

        def hold(eng, s):
            if not isinstance(s, int):
                eng.sem_inc(held, 1)

        LAYER_NORMS = 5
        NORM_STEPS = (1, 8, 14, 21, 25)
        SMALL_LOADS = [(attn_w_sb, attn_w), (wi_sb, wi_aug), (wo_ffn_sb, wo_ffn), (bo_sb, bo), (qkv_sb, qkv_aug),
                       (gb_sb, norm_gb), (fc1_sb, fc1_aug), (fc2_sb, fc2), (bfc2_sb, bfc2), (wq_pk_sb, wq_pk),
                       (wq_sb, wq), (wo_sb, wo)]
        N_LOADED = 16 * (len(SMALL_LOADS) + 2 * HEADS)

        block = ctx.enter_context(nc.Block())

        @block.sync
        def _(sp):
            sp.dma_start(C[:, :], const).then_inc(const_loaded, 16)
            sp.dma_start(ids[:, :], x).then_inc(ids_loaded, 16)
            sp.dma_start(route_i[:, :], route.partition_broadcast(128)).then_inc(ids_loaded, 16)
            for dst, src in ((wr_sb, wr), (br_sb[:], br), (ws_sb[:], ws), (bs_sb[:], bs)):
                sp.dma_start(dst, src).then_inc(experts_loaded, 16)
            for dst, src in SMALL_LOADS:
                sp.dma_start(dst[:], src).then_inc(loaded, 16)
            sp.dma_start(key_no_f[:, :, :], key_no.rearrange("p (k r) -> p k r", k=KEYS)).then_inc(tables_loaded, 16)
            sp.dma_start(sel_sb[:, :, :], sel.rearrange("k (c p) -> k c p", p=128)).then_inc(tables_loaded, 16)
            for d in range(DENSE):
                head_table = kv_table[(GATHERED + d) * KEYS * KEYS:(GATHERED + d + 1) * KEYS * KEYS, :]
                sp.dma_start(table[:, d, :, :], head_table.rearrange("(c p) d -> p c d", p=128)).then_inc(tables_loaded, 16)
            sp.wait_ge(keys_cleared, 1)
            for half in range(2):
                for h in range(HEADS):
                    q = h % 4
                    sp.dma_start(keys_sb[q * KEY_DIM:(q + 1) * KEY_DIM, half * 2 + h // 4, q, :],
                                 pk_keys[half, h, :, :]).then_inc(loaded, 16)
            sp.wait_ge(experts_ready, 1)
            sp.dma_start(expert_table.rearrange("(e p) c -> p e c", p=128), experts).then_inc(experts_stored, 16)

            def store(s):
                sp.wait_ge(out_ready, s + 1)
                hold(sp, s)
                sp.dma_start(out[bass.ds(s, 1), :, :].rearrange("a t d -> t (a d)"), out_sb[:, :]).then_inc(out_stored, 16)

            with sp.Fori(0, SEQS) as s:
                store(s)
            sp.wait_ge(out_stored, 16 * SEQS)
            sp.wait_ge(experts_stored, 16)

        @block.gpsimd
        def _(pool):
            def gather(dst, table, index):
                return nc.gpsimd.indirect_dma_start(out=dst, out_offset=None, in_=table,
                                                    in_offset=bass.IndirectOffsetOnAxis(ap=index, axis=0))

            def token_rows(s, first=False):
                pool.wait_ge(cur_ready, s + 1)
                hold(pool, s)
                if not first:
                    pool.wait_ge(emb_used, s)
                    hold(pool, s)
                    pool.wait_ge(ffn_ps_ready, s)
                    hold(pool, s)
                for n, table in enumerate((emb2, emb3, emb4)):
                    gather(emb[:, n, :], table, index_cur[:, n:n + 1]).then_inc(emb_loaded, 16)
                gather(expert_w[:, :], expert_table, index_cur[:, 3:4]).then_inc(expert_arrived, 16)

            def head_rows(s, h):
                pool.wait_ge(index_ready, s * GATHERED + h + 1)
                hold(pool, s)
                for k in range(TOP):
                    gather(rows[:, h, k, :], kv_table, row_index[:, h, k:k + 1]).then_inc(rows_loaded[h], 16)

            pool.wait_ge(experts_stored, 16)
            token_rows(0, first=True)
            token_rows(1)
            for h in range(GATHERED):
                head_rows(0, h)
            token_rows(2)
            with pool.Fori(0, SEQS - 2) as i:
                for h in range(GATHERED):
                    pool.wait_ge(kv_done, i * GATHERED + h + 1)
                    hold(pool, i)
                    head_rows(i + 1, h)
                    if h == GATHERED // 2 - 1:
                        token_rows(i + 3)
            for h in range(GATHERED):
                pool.wait_ge(kv_done, (SEQS - 2) * GATHERED + h + 1)
                head_rows(SEQS - 1, h)
            pool.wait_ge(emb_loaded, 48 * (SEQS + 1))
            pool.wait_ge(expert_arrived, 16 * (SEQS + 1))


        def dense_head(s, t):
            return (0, s, t) if t < GROUPS else (1, s + 1, t - GROUPS)

        def group_count(s, t):
            return s * 2 * GROUPS + t + GROUPS + 1

        class Kv:
            def __init__(self, s, h):
                if h < GATHERED:
                    self.ps, self.done, self.count = kv_ps[:, 128 * (h % 2):128 * (h % 2) + TOK], kv_done, s * GATHERED + h + 1
                else:
                    d = h - GATHERED
                    self.ps, self.done, self.count = dense_ps[:, 128 * d:128 * d + TOK], dense_done[d], s + 1

        @block.scalar
        def _(act):
            def copy(dst, src):
                return nc.scalar.activation(dst, src, ACT.Copy)

            def exp_and_log():
                nc.scalar.preload_act_table_set("natural_log_exp_and_others")

            def layer_rstd(s, n):
                act.wait_ge(var_ready, s * LAYER_NORMS + n + 1)
                hold(act, s)
                nc.scalar.activation(lnvar[:, :], mv[:, 1:2], ACT.Ln, bias=eps)
                nc.scalar.activation(var_eps[:, :], mv[:, 1:2], ACT.Identity, bias=eps)
                act.drain()
                nc.scalar.activation(root[:, :], lnvar[:, :], ACT.Exp, scale=-0.5)
                act.drain()
                nc.scalar.activation(root_v[:, :], root[:, :], ACT.Copy, scale=var_eps[:, :])
                nc.scalar.activation(neg_half[:, :], root[:, :], ACT.Copy, scale=-0.5)
                act.drain()
                nc.scalar.activation(factor[:, :], root_v[:, :], ACT.Identity, scale=neg_half[:, :], bias=one_and_half)
                act.drain()
                nc.scalar.activation(rstd[:, :], factor[:, :], ACT.Copy, scale=root[:, :]).then_inc(rstd_ready, 1)

            def transposed(s, n):
                act.wait_ge(xnT_ps_ready, s * LAYER_NORMS + n + 1)
                hold(act, s)
                copy(xnT[0:DIM, :], front_a[0:DIM, 0:TOK]).then_inc(xnT_ready, 1)

            def front(s, step):
                if step == 0:
                    layer_rstd(s, 0)
                elif step == 1:
                    transposed(s, 0)
                elif step == 2:
                    act.wait_ge(qkv_ps_ready, s + 1)
                    hold(act, s)
                    copy(qkT[:, :, :], front_b[0:DIM, 0:2 * TOK].rearrange("p (a t) -> p a t", a=2))
                    copy(v0[:, :], front_b[:, 256:256 + DIM]).then_inc(qkv_ready, 1)
                elif step == 4:
                    act.wait_ge(negmax_ready, s + 1)
                    hold(act, s)
                    nc.scalar.activation(probs[:, :], front_a[:, 128:256], ACT.Exp, bias=negmax[:, :],
                                         scale=DIM ** -0.5, accum_out=rowsum[:, :]).then_inc(probs_ready, 1)
                elif step == 5:
                    act.wait_ge(pT_ps_ready, s + 1)
                    hold(act, s)
                    copy(probsT[:, :], front_a[:, 0:TOK]).then_inc(pT_ready, 1)
                elif step == 7:
                    layer_rstd(s, 1)
                elif step == 8:
                    transposed(s, 1)
                elif step in (9, 10, 11):
                    n = step - 9
                    act.wait_ge(hid_ps_ready, 3 * s + n + 1)
                    hold(act, s)
                    bias = {} if n == 0 else {"bias": expert_w[:, 2 * HID + n - 1:2 * HID + n]}
                    nc.scalar.activation(hidT[:, n, :], front_b[:, 128 * n:128 * n + 128], ACT.Relu, **bias).then_inc(hid_ready, 1)
                elif step == 13:
                    layer_rstd(s, 2)
                elif step == 14:
                    transposed(s, 2)
                elif step == 15:
                    act.wait_ge(qkv1_ps_ready, s + 1)
                    hold(act, s)
                    copy(kv1[:, :], front_b[:, 0:128])
                    copy(q1T[:, :], front_b[0:DIM, 128:256]).then_inc(qkv1_ready, 1)
                elif step == 17:
                    act.wait_ge(mixmax_ready, s + 1)
                    hold(act, s)
                    nc.scalar.activation(mix[:, :], front_a[0:DIM, 128:128 + DIM], ACT.Exp, bias=negmax[0:DIM, :],
                                         scale=HEAD_DIM ** -0.5, accum_out=rowsum[0:DIM, :]).then_inc(mix_ready, 1)
                elif step == 18:
                    act.wait_ge(mixT_ps_ready, s + 1)
                    hold(act, s)
                    copy(mixT[:, :], front_a[0:DIM, 0:DIM]).then_inc(mixT_ready, 1)
                elif step == 20:
                    layer_rstd(s, 3)
                elif step == 21:
                    act.wait_ge(xnT_ps_ready, s * LAYER_NORMS + 4)
                    hold(act, s)
                    nc.scalar.activation(xnT[0:DIM, :], front_a[0:DIM, 0:TOK], ACT.Identity, bias=gb_sb[:, 1:2],
                                         scale=gb_sb[:, 0:1]).then_inc(xnT_ready, 1)
                elif step == 22:
                    act.wait_ge(fc1_ps_ready, s + 1)
                    hold(act, s)
                    nc.scalar.activation(geluT[:, :, :], front_b[0:MLP_HALF, 0:256].rearrange("p (a t) -> p a t", a=2),
                                         ACT.Gelu).then_inc(gelu_ready, 1)
                    exp_and_log()
                elif step == 24:
                    layer_rstd(s, 4)
                elif step == 25:
                    transposed(s, 4)
                elif step == 26:
                    act.wait_ge(qpk_ps_ready, s + 1)
                    hold(act, s)
                    copy(qpkT[:, :, :], front_b[:, :].rearrange("p (a t) -> p a t", a=4)).then_inc(qpk_ready, 1)
                elif step in (29, 31):
                    b = (step - 29) // 2
                    if b == 0 and (not isinstance(s, int) or s > 0):
                        act.wait_ge(sims_used, s)
                        hold(act, s)
                    act.wait_ge(sim_ps_ready, 2 * s + b + 1)
                    hold(act, s)
                    copy(sims[:, 8 * b:8 * b + 8, :], sim_ps[:, :].rearrange("p (a t) -> p a t", a=8)).then_inc(sims_ready, 1)

            def select(s, u, step):
                h = UNITS[u]
                if step == 2:
                    act.wait_ge(best_ready, s * HEADS + u + 1)
                    hold(act, s)
                    last = nc.scalar.activation(expbest[:, :], best[:, :], ACT.Exp, bias=negbest[:, :],
                                                accum_out=expsum[:, :])
                    if h >= GATHERED:
                        act.drain()
                        last = nc.scalar.activation(lnsum[:, :], expsum[:, :], ACT.Ln)
                    last.then_inc(expbest_ready, 1)

            def codes(s, u):
                h = UNITS[u - 1]
                if h >= GATHERED:
                    act.wait_ge(code_ps_ready, s * DENSE + (h == HEAD_A) + 1)
                    hold(act, s)
                    copy(scoreT[:, h - GATHERED, :], code_ps[h][:, 0:TOK])
                    copy(codeT[:, h - GATHERED, :], code_ps[h][:, TOK:2 * TOK]).then_inc(codeT_ready, 1)

            def dense(s, t):
                act.wait_ge(pair_ps_ready, group_count(s, t))
                hold(act, s)
                nc.scalar.activation(pair_exp[:, t % 2, :], pair_ps[t % 2][:, 0:GROUP_COLS], ACT.Exp).then_inc(pair_exp_ready, 1)

            def diagonals(s, h, step, steps=STEPS):
                if step == 0:
                    act.wait_ge(weight_ready, s * GATHERED + h + 1)
                    hold(act, s)
                    if h >= 2:
                        act.wait_ge(kv_done, s * GATHERED + h - 1)
                        hold(act, s)
                for k in range(TOP // steps * step, TOP // steps * (step + 1)):
                    last = nc.scalar.activation(diag[:, h % 2, k, :], ident, ACT.Copy, scale=weight[:, h, k:k + 1])
                if step == steps - 1:
                    last.then_inc(diag_ready, 1)

            def back(s, u, stage):
                n = s * HEADS + u
                p = u % 2
                if stage == 1:
                    kv = Kv(s, UNITS[u])
                    act.wait_ge(kv.done, kv.count)
                    hold(act, s)
                    act.wait_ge(q_ps_ready, n + 1)
                    hold(act, s)
                    copy(kvT[p][:, :], kv.ps)
                    copy(qhT[p][:, :], turn_ps[p][0:DIM, 384:512]).then_inc(kvT_ready, 1)
                elif stage == 2:
                    act.wait_ge(v_ready, n + 1)
                    hold(act, s)
                    copy(v_rows[p][:, :], turn_ps[p][:, DIM:2 * DIM]).then_inc(v_copied, 1)
                elif stage == 3:
                    act.wait_ge(b_neg_ready, n + 1)
                    hold(act, s)
                    nc.scalar.activation(b_probs[p][:, :], score_ps[p], ACT.Exp, bias=b_neg[p][:, :],
                                         scale=DIM ** -0.5, accum_out=b_sum[p][:, :]).then_inc(b_probs_ready, 1)

            def unit_diagonals(s, u, step, last_seq=False):
                if u in DIAGONALS_AT:
                    h = DIAGONALS_AT[u]
                    if h > 0:
                        diagonals(s, h, step)
                    elif not last_seq:
                        act.wait_ge(kv_done, s * GATHERED + GATHERED - 1)
                        hold(act, s)
                        diagonals(s + 1, h, step)

            exp_and_log()
            act.wait_ge(const_loaded, 16)
            act.wait_ge(loaded, N_LOADED)
            for step in range(FRONT_STEPS):
                front(0, step)
            for u in range(HEADS):
                for step in range(STEPS):
                    if u > 0 and step == 0:
                        codes(0, u)
                    front(1, u * STEPS + step)
                    select(0, u, step)
            diagonals(0, 0, 0, steps=1)
            for t in range(GROUPS, 2 * GROUPS):
                dense(-1, t)
            with act.Fori(0, SEQS - 2) as i:
                for u in range(HEADS):
                    for step in range(STEPS):
                        if u > 0 and step == 0:
                            codes(i + 1, u)
                        back(i, u, step)
                        dense(i, u * STEPS + step)
                        select(i + 1, u, step)
                        unit_diagonals(i, u, step)
                        front(i + 2, u * STEPS + step)
            for u in range(HEADS):
                for step in range(STEPS):
                    if u > 0 and step == 0:
                        codes(SEQS - 1, u)
                    back(SEQS - 2, u, step)
                    dense(SEQS - 2, u * STEPS + step)
                    select(SEQS - 1, u, step)
                    unit_diagonals(SEQS - 2, u, step)
            for u in range(HEADS):
                for step in range(STEPS):
                    back(SEQS - 1, u, step)
                    if u * STEPS + step < GROUPS:
                        dense(SEQS - 1, u * STEPS + step)
                    unit_diagonals(SEQS - 1, u, step, last_seq=True)

        @block.vector
        def _(dve):
            v = nc.vector

            def moments(src):
                dve.drain()
                v.bn_stats(stats[:, :], src)
                dve.drain()
                v.bn_aggr(mv[:, :], stats[:, :]).then_inc(var_ready, 1)

            def normalize(s, n, src, dst):
                dve.wait_ge(rstd_ready, s * LAYER_NORMS + n + 1)
                hold(dve, s)
                v.tensor_scalar(dst, src, mv[:, 0:1], rstd[:, :], ALU.subtract, ALU.mult).then_inc(xn_ready, 1)

            def negated_max(scores, high, low, scale):
                v.reduce_max(high, scores, AX.X)
                dve.drain()
                return v.tensor_scalar(low, high, -scale, None, ALU.mult)

            def front(s, step):
                if step == 0:
                    dve.wait_ge(emb_loaded, 48 * s + 48)
                    hold(dve, s)
                    dve.wait_ge(expert_arrived, 16 * s + 16)
                    hold(dve, s)
                    v.tensor_copy(index_cur[:, :], index_all[:, bass.ds(s + 1, 1), :].rearrange("p a c -> p (a c)")).then_inc(cur_ready, 1)
                    v.tensor_scalar(h0[:, :], emb[:, 0, :], C[:, C_GRAM:C_GRAM + 1], None, ALU.mult)
                    dve.drain()
                    v.scalar_tensor_tensor(h0[:, :], emb[:, 1, :], C[:, C_GRAM + 1:C_GRAM + 2], h0[:, :], ALU.mult, ALU.add)
                    dve.drain()
                    v.scalar_tensor_tensor(h0[:, :], emb[:, 2, :], C[:, C_GRAM + 2:C_GRAM + 3], h0[:, :], ALU.mult, ALU.add).then_inc(emb_used, 1)
                    moments(h0[:, :])
                elif step == 1:
                    normalize(s, 0, h0[:, :], xn[:, :])
                elif step == 4:
                    dve.wait_ge(scores_ready, s + 1)
                    hold(dve, s)
                    negated_max(front_a[:, 128:256], rowmax[:, :], negmax[:, :], DIM ** -0.5).then_inc(negmax_ready, 1)
                elif step == 7:
                    dve.wait_ge(probs_ready, s + 1)
                    hold(dve, s)
                    v.reciprocal(rsum[:, :], rowsum[:, :])
                    dve.drain()
                    dve.wait_ge(attn_ps_ready, s + 1)
                    hold(dve, s)
                    v.scalar_tensor_tensor(h1[:, :], front_b[:, 384:384 + DIM], rsum[:, :], h0[:, :], ALU.mult, ALU.add)
                    moments(h1[:, :])
                elif step == 8:
                    normalize(s, 1, h1[:, :], xn[:, :])
                elif step == 13:
                    dve.wait_ge(ffn_ps_ready, s + 1)
                    hold(dve, s)
                    v.tensor_tensor(h2[:, :], h1[:, :], front_a[:, 384:384 + DIM], ALU.add)
                    moments(h2[:, :])
                elif step == 14:
                    normalize(s, 2, h2[:, :], x2[:, :])
                elif step == 17:
                    dve.wait_ge(mix_ps_ready, s + 1)
                    hold(dve, s)
                    negated_max(front_a[0:DIM, 128:128 + DIM], rowmax[0:DIM, :], negmax[0:DIM, :], HEAD_DIM ** -0.5).then_inc(mixmax_ready, 1)
                elif step == 18:
                    dve.wait_ge(mix_ready, s + 1)
                    hold(dve, s)
                    v.reciprocal(rsum[0:DIM, :], rowsum[0:DIM, :])
                    dve.drain()
                    v.tensor_scalar(mixn[:, :], mix[:, :], rsum[0:DIM, :], None, ALU.mult).then_inc(mixn_ready, 1)
                elif step == 20:
                    dve.wait_ge(xf_ps_ready, s + 1)
                    hold(dve, s)
                    v.tensor_tensor(x3[:, :], x2[:, :], front_a[:, 384:384 + DIM], ALU.add)
                    moments(x3[:, :])
                elif step == 21:
                    normalize(s, 3, x3[:, :], xn[:, :])
                elif step == 24:
                    dve.wait_ge(mlp_ps_ready, s + 1)
                    hold(dve, s)
                    v.tensor_tensor(mlp_sum[:, :], x3[:, :], front_b[:, 384:384 + DIM], ALU.add)
                    dve.drain()
                    v.tensor_tensor(h3[:, :], h2[:, :], mlp_sum[:, :], ALU.add)
                    moments(h3[:, :])
                elif step == 25:
                    normalize(s, 4, h3[:, :], xn[:, :])

            def dense(s, t):
                dve.wait_ge(pair_exp_ready, group_count(s, t))
                hold(dve, s)
                v.scalar_tensor_tensor(pair_weight[:, t % 2, :], pair_ps[t % 2][:, GROUP_COLS:2 * GROUP_COLS],
                                       float(-NOT_RANKED), pair_exp[:, t % 2, :], ALU.is_lt, ALU.mult).then_inc(pair_weight_ready, 1)

            def select(s, u, step):
                n = s * HEADS + u
                h = UNITS[u]
                part = [sims[:, h, :], sims[:, HEADS + h, :]]
                if step == 0:
                    if u == 0:
                        dve.wait_ge(sims_ready, 2 * s + 2)
                        hold(dve, s)
                    for a in range(2):
                        v.max(top[:, a, 0, 0:8], part[a])
                    dve.drain()
                    for a in range(2):
                        v.max_index(pos[:, a, 0:8], top[:, a, 0, 0:8], part[a])
                    for a in range(2):
                        last = v.match_replace(rest[:, a, :], top[:, a, 0, 0:8], part[a], REPLACED)
                    if u == HEADS - 1:
                        last.then_inc(sims_used, 1)
                    dve.drain()
                    for a in range(2):
                        v.max(top[:, a, 0, 8:16], rest[:, a, :])
                    dve.drain()
                    for a in range(2):
                        v.max_index(pos[:, a, 8:16], top[:, a, 0, 8:16], rest[:, a, :])
                elif step == 1:
                    dve.drain()
                    sums = 1
                    if h < GATHERED:
                        sums = 2
                        v.tensor_scalar(top[:, 0, 1, :], pos[:, 0, :], float(h * KEYS * KEYS), None, ALU.add)
                        v.tensor_scalar(top[:, 1, 1, :], pos[:, 1, :], float(KEYS), None, ALU.mult)
                        dve.drain()
                    else:
                        v.tensor_copy(pos_bf[:, :, :], pos[:, :, :])
                    at = 0
                    for i0, ni, nj in STAIRS:
                        v.tensor_tensor(pairs[:, 0:sums, at:at + ni * nj].rearrange("p a (i j) -> p a i j", i=ni),
                                        top[:, 0, 0:sums, i0:i0 + ni].unsqueeze(3).broadcast_to([TOK, sums, ni, nj]),
                                        top[:, 1, 0:sums, 0:nj].unsqueeze(2).broadcast_to([TOK, sums, ni, nj]), ALU.add)
                        at += ni * nj
                    dve.drain()
                    v.max(best[:, 0:8], pairs[:, 0, :])
                    dve.drain()
                    v.tensor_scalar(negbest[:, :], best[:, 0:1], -1.0, None, ALU.mult)
                    if h < GATHERED:
                        v.max_index(best_pos[:, 0:8], best[:, 0:8], pairs[:, 0, :])
                    v.match_replace(pairs_rest[:, :], best[:, 0:8], pairs[:, 0, :], REPLACED)
                    dve.drain()
                    v.max(best[:, 8:16], pairs_rest[:, :]).then_inc(best_ready, 1)
                elif h < GATHERED:
                    select_rows(s, h, n, step)
                else:
                    select_codes(s, h, n, step)

            def select_rows(s, h, n, step):
                if step == 2:
                    dve.drain()
                    v.max_index(best_pos[:, 8:16], best[:, 8:16], pairs_rest[:, :])
                    dve.drain()
                    v.tensor_tensor(onehot[:, :, :], best_pos[:, :].unsqueeze(2).broadcast_to([TOK, TOP, PAIRS]),
                                    iota.unsqueeze(1).broadcast_to([TOK, TOP, PAIRS]), ALU.is_equal)
                    dve.drain()
                    v.tensor_tensor(onehot[:, :, :], onehot[:, :, :], pairs[:, 1, :].unsqueeze(1).broadcast_to([TOK, TOP, PAIRS]), ALU.mult)
                elif step == 3:
                    dve.drain()
                    with nc.allow_low_precision(reason="one row number and zeros: exact"):
                        v.tensor_reduce(row_index[:, h, :], onehot[:, :, :], AX.X, ALU.add).then_inc(index_ready, 1)
                    dve.wait_ge(expbest_ready, n + 1)
                    hold(dve, s)
                    v.reciprocal(rexp[:, :], expsum[:, :])
                    dve.drain()
                    v.tensor_scalar(weight[:, h, :], expbest[:, :], rexp[:, :], None, ALU.mult).then_inc(weight_ready, 1)

            def select_codes(s, h, n, step):
                if step == 2:
                    dve.drain()
                    v.match_replace(pairs[:, 0, :], best[:, 8:16], pairs_rest[:, :], REPLACED)
                    dve.drain()
                    v.tensor_scalar(selected[:, :], pairs[:, 0, :], REPLACED, -1.0, ALU.is_equal, ALU.mult)
                    dve.drain()
                    at = 0
                    for i0, ni, nj in STAIRS:
                        with nc.allow_low_precision(reason="counts up to 16: exact"):
                            v.tensor_reduce(rank_code[:, 0, i0:i0 + ni], selected[:, at:at + ni * nj].rearrange("p (i j) -> p i j", i=ni),
                                            AX.X, ALU.add)
                        at += ni * nj
                    v.tensor_tensor(key_hot[:, :, :, :], pos_bf[:, :, :].unsqueeze(2).broadcast_to([TOK, 2, KEYS, TOP]),
                                    key_no_bf[:, :, :].unsqueeze(1).broadcast_to([TOK, 2, KEYS, TOP]), ALU.is_equal)
                    dve.drain()
                    v.tensor_tensor(key_hot[:, :, :, :], key_hot[:, :, :, :],
                                    rank_code[:, :, :].unsqueeze(2).broadcast_to([TOK, 2, KEYS, TOP]), ALU.mult)
                elif step == 3:
                    dve.drain()
                    v.tensor_reduce(key_code[:, :, :], key_hot[:, :, :, :], AX.X, ALU.add)
                    dve.wait_ge(expbest_ready, n + 1)
                    hold(dve, s)
                    v.tensor_tensor(shift[:, :], negbest[:, :], lnsum[:, :], ALU.subtract)
                    dve.drain()
                    v.tensor_scalar(key_score[:, 0, :], sims[:, h, :], shift[:, :], None, ALU.add)
                    v.tensor_copy(key_score[:, 1, :], sims[:, HEADS + h, :])
                    dve.drain().then_inc(score_code_ready, 1)

            def add_head(s, u):
                dve.wait_ge(y_ps_ready, s * HEADS + u + 1)
                hold(dve, s)
                if u == HEADS - 1:
                    dve.drain()
                    v.tensor_tensor(out_sb[:, :], y_sum[:, :], y_ps[u % 2], ALU.add).then_inc(out_ready, 1)
                else:
                    v.tensor_tensor(y_sum[:, :], h3_cur[:, :] if u == 0 else y_sum[:, :], y_ps[u % 2], ALU.add).then_inc(y_added, 1)

            def back(s, u, stage):
                n = s * HEADS + u
                p = u % 2
                if stage == 2:
                    dve.wait_ge(v_copied, n + 1)
                    hold(dve, s)
                    negated_max(score_ps[p], b_max[p][:, :], b_neg[p][:, :], DIM ** -0.5).then_inc(b_neg_ready, 1)
                elif stage == 3:
                    dve.wait_ge(b_probs_ready, n + 1)
                    hold(dve, s)
                    v.reciprocal(b_rsum[p][:, :], b_sum[p][:, :])
                    dve.drain()
                    v.tensor_scalar(b_norm[p][:, :], b_probs[p][:, :], b_rsum[p][:, :], None, ALU.mult).then_inc(b_norm_ready, 1)
                elif stage == 4:
                    dve.wait_ge(b_pT_ps_ready, n + 1)
                    hold(dve, s)
                    v.tensor_copy(b_probsT[p][:, :], turn_ps[p][:, 128:256]).then_inc(b_pT_ready, 1)
                elif stage == 5:
                    dve.wait_ge(headT_ps_ready, n + 1)
                    hold(dve, s)
                    v.tensor_copy(headT[p][:, :], turn_ps[p][0:DIM, 256:384]).then_inc(headT_ready, 1)
                elif stage == 6:
                    add_head(s, u)

            def backs(s, u, step):
                if u > 0:
                    back(s, u - 1, step + STEPS)
                elif not isinstance(s, int) or s > 0:
                    back(s - 1, HEADS - 1, step + STEPS)
                back(s, u, step)

            def back_end(s):
                for stage in range(STEPS, STEPS + 3):
                    back(s, HEADS - 1, stage)

            def out_free(s):
                if not isinstance(s, int) or s > 0:
                    dve.wait_ge(out_stored, 16 * s)
                    hold(dve, s)

            def carry(first=False):
                if not first:
                    v.tensor_copy(h3_cur[:, :], h3_next[:, :])
                    v.tensor_copy(x4T_cur[:, :], x4T_next[:, :]).then_inc(carried, 1)
                    dve.drain()
                v.tensor_copy(h3_next[:, :], h3[:, :])
                v.tensor_copy(x4T_next[:, :], x4T).then_inc(x4T_used, 1)

            v.memset(keys_sb[:], 0.0).then_inc(keys_cleared, 1)
            v.memset(ones_row[:, :], 1.0)
            v.memset(xnT[DIM:DIM + 1, :], 1.0).then_inc(consts_set, 1)
            v.memset(hashes[:], 0.0)
            v.memset(index_all[:], 0)
            dve.wait_ge(ids_loaded, 32)
            v.tensor_copy(idf[:, :], ids[:, :])
            v.tensor_copy(route_f[:, :], route_i[:, :])
            dve.drain()
            for n, g in enumerate(GRAMS):
                back_by = g - 1
                newer = idf[:, back_by:] if n == 0 else hashes[:, n - 1, back_by:]
                v.scalar_tensor_tensor(hashes[:, n, back_by:], idf[:, 0:TOK - back_by], float(PRIME ** back_by % VOCAB),
                                       newer, ALU.mult, ALU.add)
                dve.drain()
            v.tensor_scalar(quot_i[:], hashes[:], 1.0 / VOCAB, None, ALU.mult)
            dve.drain()
            v.tensor_copy(quot[:], quot_i[:])
            dve.drain()
            v.scalar_tensor_tensor(hashes[:], quot[:], float(-VOCAB), hashes[:], ALU.mult, ALU.add)
            dve.drain()
            v.tensor_scalar(quot[:], hashes[:], 0.0, float(VOCAB), ALU.is_lt, ALU.mult)
            dve.drain()
            v.tensor_tensor(hashes[:], hashes[:], quot[:], ALU.add)
            dve.drain()
            v.tensor_scalar(quot[:], hashes[:], float(VOCAB), float(-VOCAB), ALU.is_ge, ALU.mult)
            dve.drain()
            v.tensor_tensor(hashes[:], hashes[:], quot[:], ALU.add).then_inc(hashed, 1)
            dve.wait_ge(const_loaded, 16)
            v.tensor_scalar(route_ok[:, :], route_f[:, :], 0.0, None, ALU.is_ge)
            dve.drain()
            v.scalar_tensor_tensor(route_ok[:, :], route_f[:, :], float(EXPERTS - 1), route_ok[:, :], ALU.is_le, ALU.mult)
            dve.drain()
            v.scalar_tensor_tensor(route_f[:, :], route_f[:, :], float(-EXPERTS), route_ok[:, :], ALU.add, ALU.mult)
            dve.drain()
            v.tensor_scalar(route_f[:, :], route_f[:, :], float(EXPERTS), 128.0, ALU.add, ALU.mult)
            dve.drain()
            v.tensor_scalar(index_all[:, 0:SEQS, 3].rearrange("p (g s) -> p g s", s=GROUP),
                            route_f[:, :].unsqueeze(2).broadcast_to([128, ROUTES, GROUP]),
                            C[:, C_PART:C_PART + 1], None, ALU.add)
            dve.wait_ge(hashT_ready, 1)
            v.tensor_copy(index_all[:, 0:SEQS, 0:3], front_a[:, 0:384].rearrange("p (n s) -> p s n", n=3))
            dve.drain()
            v.tensor_copy(index_cur[:, :], index_all[:, 0, :]).then_inc(cur_ready, 1)
            dve.wait_ge(experts_loaded, 64)
            for l in range(2):
                v.tensor_tensor(ws_sb[:, l, :], ws_sb[:, l, :], ident, ALU.add)
            dve.drain()
            for l in range(2):
                cols = slice(l * HID, (l + 1) * HID)
                v.tensor_tensor(experts[:, 0:EXPERTS, cols], wr_sb[:, l, :, :],
                                ws_sb[:, l, :].unsqueeze(1).broadcast_to([HID, EXPERTS, HID]), ALU.add)
                v.tensor_copy(experts[:, EXPERTS, cols], ws_sb[:, l, :])
                v.tensor_scalar(experts[:, 0:EXPERTS, 2 * HID + l], br_sb[:, l, :], bs_sb[:, l:l + 1], None, ALU.add)
                v.tensor_copy(experts[:, EXPERTS, 2 * HID + l:2 * HID + l + 1], bs_sb[:, l:l + 1])
            dve.drain().then_inc(experts_ready, 1)

            for step in range(FRONT_STEPS):
                front(0, step)
            dve.wait_ge(qpk_ps_ready, 1)
            carry(first=True)
            dve.wait_ge(tables_loaded, 16 * (2 + DENSE))
            v.tensor_copy(key_no_bf[:], key_no_f[:])
            v.tensor_copy(sel_bf[:], sel_sb[:])
            for r in range(TOP):
                v.memset(rank_code[:, 1, r:r + 1], float(r - NOT_RANKED))
            dve.drain().then_inc(dense_set, 1)
            for u in range(HEADS):
                for step in range(STEPS):
                    front(1, u * STEPS + step)
                    select(0, u, step)
            dve.wait_ge(qpk_ps_ready, 2)
            carry()
            for t in range(GROUPS, 2 * GROUPS):
                dense(-1, t)

            def body(i):
                for u in range(HEADS):
                    for step in range(STEPS):
                        late = u * STEPS + step in NORM_STEPS
                        if not late:
                            front(i + 2, u * STEPS + step)
                        select(i + 1, u, step)
                        if late:
                            front(i + 2, u * STEPS + step)
                        backs(i, u, step)
                        dense(i, u * STEPS + step)
                dve.wait_ge(qpk_ps_ready, i + 3)
                hold(dve, i)
                out_free(i)
                carry()

            body(0)
            with dve.Fori(1, SEQS - 2) as i:
                body(i)
            for u in range(HEADS):
                for step in range(STEPS):
                    select(SEQS - 1, u, step)
                    backs(SEQS - 2, u, step)
                    dense(SEQS - 2, u * STEPS + step)
            out_free(SEQS - 2)
            carry()
            for u in range(HEADS):
                for step in range(STEPS):
                    backs(SEQS - 1, u, step)
                    if u * STEPS + step < GROUPS:
                        dense(SEQS - 1, u * STEPS + step)
            out_free(SEQS - 1)
            back_end(SEQS - 1)

        @block.tensor
        def _(pe):
            mm = nc.tensor.matmul

            def transpose_norm(s, n, src):
                pe.wait_ge(xn_ready, s * LAYER_NORMS + n + 1)
                hold(pe, s)
                nc.tensor.transpose(front_a[0:DIM, 0:TOK], src, ident).then_inc(xnT_ps_ready, 1)

            def front(s, step):
                if step == 1:
                    if not isinstance(s, int) or s > 0:
                        pe.wait_ge(x4T_used, s)
                        hold(pe, s)
                    transpose_norm(s, 0, xn[:, :])
                elif step == 2:
                    if not isinstance(s, int) or s > 0:
                        pe.wait_ge(sims_ready, 2 * s)
                        hold(pe, s)
                    pe.wait_ge(xnT_ready, s * LAYER_NORMS + 1)
                    hold(pe, s)
                    mm(front_b[0:DIM, 0:128], attn_w_sb[:, 0, :], xnT[:, :], start=True, stop=True)
                    mm(front_b[0:DIM, 128:256], attn_w_sb[:, 1, :], xnT[:, :], start=True, stop=True)
                    mm(front_b[:, 256:256 + DIM], xnT[:, :], attn_w_sb[:, 2, :], start=True, stop=True).then_inc(qkv_ps_ready, 1)
                elif step == 3:
                    pe.wait_ge(qkv_ready, s + 1)
                    hold(pe, s)
                    mm(front_a[:, 128:256], qkT[:, 0, :], qkT[:, 1, :], start=True, stop=True).then_inc(scores_ready, 1)
                elif step == 5:
                    pe.wait_ge(probs_ready, s + 1)
                    hold(pe, s)
                    nc.tensor.transpose(front_a[:, 0:TOK], probs[:, :], ident).then_inc(pT_ps_ready, 1)
                elif step == 6:
                    if not isinstance(s, int) or s > 0:
                        pe.wait_ge(codeT_ready, (s - 1) * DENSE + 1)
                        hold(pe, s)
                    pe.wait_ge(pT_ready, s + 1)
                    hold(pe, s)
                    mm(front_b[:, 384:384 + DIM], probsT[:, :], v0[:, :], start=True, stop=True).then_inc(attn_ps_ready, 1)
                elif step == 8:
                    transpose_norm(s, 1, xn[:, :])
                elif step == 9:
                    pe.wait_ge(xnT_ready, s * LAYER_NORMS + 2)
                    hold(pe, s)
                    mm(front_b[:, 0:128], wi_sb[:, :], xnT[:, :], start=True, stop=True).then_inc(hid_ps_ready, 1)
                elif step in (10, 11):
                    n = step - 10
                    pe.wait_ge(hid_ready, 3 * s + n + 1)
                    hold(pe, s)
                    mm(front_b[:, 128 * (n + 1):128 * (n + 2)], expert_w[:, n * HID:(n + 1) * HID], hidT[:, n, :],
                       start=True, stop=True).then_inc(hid_ps_ready, 1)
                elif step == 12:
                    pe.wait_ge(hid_ready, 3 * s + 3)
                    hold(pe, s)
                    mm(front_a[:, 384:384 + DIM], hidT[:, 2, :], wo_ffn_sb[:, :], start=True, stop=False)
                    mm(front_a[:, 384:384 + DIM], ones_row[:, :], bo_sb[:, :], start=False, stop=True).then_inc(ffn_ps_ready, 1)
                elif step == 14:
                    transpose_norm(s, 2, x2[:, :])
                elif step == 15:
                    pe.wait_ge(xnT_ready, s * LAYER_NORMS + 3)
                    hold(pe, s)
                    mm(front_b[:, 0:128], xnT[:, :], qkv_sb[:, DIM:3 * DIM], start=True, stop=True)
                    mm(front_b[0:DIM, 128:256], qkv_sb[:, 0:DIM], xnT[:, :], start=True, stop=True).then_inc(qkv1_ps_ready, 1)
                elif step == 16:
                    pe.wait_ge(qkv1_ready, s + 1)
                    hold(pe, s)
                    mm(front_a[0:DIM, 128:128 + DIM], kv1[:, 0:DIM], kv1[:, DIM:2 * DIM], start=True, stop=False)
                    mm(front_a[0:DIM, 128:128 + DIM], ident[0:DIM, 0:DIM], block_mask, start=False, stop=True).then_inc(mix_ps_ready, 1)
                elif step == 18:
                    pe.wait_ge(mixn_ready, s + 1)
                    hold(pe, s)
                    nc.tensor.transpose(front_a[0:DIM, 0:DIM], mixn[:, :], ident[0:DIM, 0:DIM]).then_inc(mixT_ps_ready, 1)
                elif step == 19:
                    pe.wait_ge(mixT_ready, s + 1)
                    hold(pe, s)
                    mm(front_a[:, 384:384 + DIM], q1T[:, :], mixT[:, :], start=True, stop=True).then_inc(xf_ps_ready, 1)
                elif step == 21:
                    transpose_norm(s, 3, xn[:, :])
                elif step == 22:
                    pe.wait_ge(xnT_ready, s * LAYER_NORMS + 4)
                    hold(pe, s)
                    mm(front_b[0:MLP_HALF, 0:128], fc1_sb[:, 0:MLP_HALF], xnT[:, :], start=True, stop=True)
                    mm(front_b[0:MLP_HALF, 128:256], fc1_sb[:, MLP_HALF:MLP], xnT[:, :], start=True, stop=True).then_inc(fc1_ps_ready, 1)
                elif step == 23:
                    pe.wait_ge(gelu_ready, s + 1)
                    hold(pe, s)
                    mm(front_b[:, 384:384 + DIM], geluT[:, 0, :], fc2_sb[:, 0, :], start=True, stop=False)
                    mm(front_b[:, 384:384 + DIM], geluT[:, 1, :], fc2_sb[:, 1, :], start=False, stop=False)
                    mm(front_b[:, 384:384 + DIM], ones_row[:, :], bfc2_sb[:, :], start=False, stop=True).then_inc(mlp_ps_ready, 1)
                elif step == 25:
                    if not isinstance(s, int) or s > 0:
                        pe.wait_ge(codeT_ready, s * DENSE)
                        hold(pe, s)
                    transpose_norm(s, 4, xn[:, :])
                elif step == 26:
                    pe.wait_ge(xnT_ready, s * LAYER_NORMS + 5)
                    hold(pe, s)
                    for c in range(4):
                        last = mm(front_b[:, 128 * c:128 * c + 128], wq_pk_sb[:, 128 * c:128 * c + 128], xnT[0:DIM, :], start=True, stop=True)
                    last.then_inc(qpk_ps_ready, 1)
                elif step in (27, 30):
                    b = (step - 27) // 3
                    if b == 0:
                        pe.wait_ge(qpk_ready, s + 1)
                        hold(pe, s)
                    else:
                        pe.wait_ge(sims_ready, 2 * s + 1)
                        hold(pe, s)
                    for c in range(2):
                        last = mm(sim_ps[:, 256 * c:256 * c + 256], qpkT[:, 2 * b + c, :],
                                  keys_sb[:, 2 * b + c, :, :].rearrange("p a k -> p (a k)"), start=True, stop=True)
                    last.then_inc(sim_ps_ready, 1)

            def codes(s, u):
                h = UNITS[u - 1]
                if h >= GATHERED:
                    pe.wait_ge(score_code_ready, s * DENSE + (h == HEAD_A) + 1)
                    hold(pe, s)
                    nc.tensor.transpose(code_ps[h][:, 0:TOK], key_score[:, :, :].rearrange("p a k -> p (a k)"), ident)
                    nc.tensor.transpose(code_ps[h][:, TOK:2 * TOK], key_code[:, :, :].rearrange("p a k -> p (a k)"), ident).then_inc(code_ps_ready, 1)

            def dense_pairs(s, t):
                d, seq, g = dense_head(s, t)
                if g == 0:
                    pe.wait_ge(codeT_ready, seq * DENSE + (d == 0) + 1)
                    hold(pe, seq)
                for c in range(GROUP_SLOTS):
                    mm(pair_ps[t % 2][:, c * TOK:(c + 1) * TOK], sel_sb[:, g * GROUP_SLOTS + c, :], scoreT[:, d, :],
                       start=True, stop=True)
                for c in range(GROUP_SLOTS):
                    last = mm(pair_ps[t % 2][:, GROUP_COLS + c * TOK:GROUP_COLS + (c + 1) * TOK], sel_bf[:, g * GROUP_SLOTS + c, :],
                              codeT[:, d, :], start=True, stop=True)
                last.then_inc(pair_ps_ready, 1)

            def dense_sum(s, t):
                d, seq, g = dense_head(s, t)
                pe.wait_ge(pair_weight_ready, group_count(s, t))
                hold(pe, s)
                for c in range(GROUP_SLOTS):
                    last = mm(dense_ps[:, 128 * d:128 * d + TOK], table[:, d, g * GROUP_SLOTS + c, :],
                              pair_weight[:, t % 2, c * TOK:(c + 1) * TOK],
                              start=(g == 0 and c == 0), stop=(g == GROUPS - 1 and c == GROUP_SLOTS - 1))
                if g == GROUPS - 1:
                    last.then_inc(dense_done[d], 1)

            def dense_sum_before(s, t):
                if t > 0:
                    dense_sum(s, t - 1)
                else:
                    dense_sum(s - 1, 2 * GROUPS - 1)

            def weighted_sum(s, h, first, count):
                if first == 0:
                    pe.wait_ge(diag_ready, s * GATHERED + h + 1)
                    hold(pe, s)
                    pe.wait_ge(rows_loaded[h], 16 * TOP * s + 16 * TOP)
                    hold(pe, s)
                for k in range(first, first + count):
                    last = mm(kv_ps[:, 128 * (h % 2):128 * (h % 2) + TOK], rows[:, h, k, :], diag[:, h % 2, k, :],
                              start=(k == 0), stop=(k == TOP - 1))
                if first + count == TOP:
                    last.then_inc(kv_done, 1)

            def queries(s, u):
                n = s * HEADS + u
                h = UNITS[u]
                if u == 0:
                    pe.wait_ge(carried, s + 1)
                    hold(pe, s)
                elif u == 1:
                    if not isinstance(s, int) or s > 0:
                        pe.wait_ge(out_ready, s)
                        hold(pe, s)
                elif u > 1:
                    pe.wait_ge(y_added, s * (HEADS - 1) + u - 1)
                    hold(pe, s)
                mm(turn_ps[u % 2][0:DIM, 384:512], wq_sb[:, h * DIM:(h + 1) * DIM], x4T_cur[:, :], start=True, stop=True).then_inc(q_ps_ready, 1)

            def scores(s, u):
                p = u % 2
                pe.wait_ge(kvT_ready, s * HEADS + u + 1)
                hold(pe, s)
                nc.tensor.transpose(turn_ps[p][:, 0:2 * DIM], kvT[p][:, :], ident)
                mm(score_ps[p], qhT[p][:, :], kvT[p][0:DIM, :], start=True, stop=False)
                mm(score_ps[p], ident, causal, start=False, stop=True).then_inc(v_ready, 1)

            def back(s, u, stage):
                n = s * HEADS + u
                p = u % 2
                if stage == 4:
                    pe.wait_ge(b_norm_ready, n + 1)
                    hold(pe, s)
                    nc.tensor.transpose(turn_ps[p][:, 128:256], b_norm[p][:, :], ident).then_inc(b_pT_ps_ready, 1)
                elif stage == 5:
                    pe.wait_ge(b_pT_ready, n + 1)
                    hold(pe, s)
                    mm(turn_ps[p][0:DIM, 256:384], v_rows[p][:, :], b_probsT[p][:, :], start=True, stop=True).then_inc(headT_ps_ready, 1)
                elif stage == 6:
                    pe.wait_ge(headT_ready, n + 1)
                    hold(pe, s)
                    mm(y_ps[p], headT[p][:, :], wo_sb[:, UNITS[u], :], start=True, stop=True).then_inc(y_ps_ready, 1)

            def step_start(s, u, step):
                if u > 0:
                    back(s, u - 1, step + STEPS)
                elif not isinstance(s, int) or s > 0:
                    back(s - 1, HEADS - 1, step + STEPS)
                if u == 0 and step == 0:
                    dense_sum_before(s, 0)

            def step_end(s, u, step):
                t = u * STEPS + step
                if step == 1:
                    scores(s, u)
                if t > 0 and (not isinstance(s, int) or s < SEQS - 1 or t <= GROUPS):
                    dense_sum_before(s, t)
                if step == 0:
                    queries(s, u)
                if step >= 2 and u in SUMS_AT:
                    weighted_sum(s, SUMS_AT[u], (step - 2) * TOP // 2, TOP // 2)

            def back_end(s):
                for stage in range(STEPS, STEPS + 3):
                    back(s, HEADS - 1, stage)

            pe.wait_ge(const_loaded, 16)
            pe.wait_ge(hashed, 1)
            for n in range(3):
                last = nc.tensor.transpose(front_a[:, 128 * n:128 * n + 128], hashes[:, n, :], ident)
            last.then_inc(hashT_ready, 1)
            pe.wait_ge(loaded, N_LOADED)
            pe.wait_ge(consts_set, 1)
            for step in range(FRONT_STEPS):
                front(0, step)
            for u in range(HEADS):
                for step in range(STEPS):
                    if u > 0 and step == 0:
                        codes(0, u)
                    front(1, u * STEPS + step)
            pe.wait_ge(dense_set, 1)
            pe.wait_ge(tables_loaded, 16 * (2 + DENSE))
            for t in range(GROUPS, 2 * GROUPS):
                dense_pairs(-1, t)
                if t > GROUPS:
                    dense_sum_before(-1, t)

            def body(i):
                for u in range(HEADS):
                    for step in range(STEPS):
                        if u > 0 and step == 0:
                            codes(i + 1, u)
                        step_start(i, u, step)
                        dense_pairs(i, u * STEPS + step)
                        step_end(i, u, step)
                        front(i + 2, u * STEPS + step)

            body(0)
            with pe.Fori(1, SEQS - 2) as i:
                body(i)
            for u in range(HEADS):
                for step in range(STEPS):
                    if u > 0 and step == 0:
                        codes(SEQS - 1, u)
                    step_start(SEQS - 2, u, step)
                    dense_pairs(SEQS - 2, u * STEPS + step)
                    step_end(SEQS - 2, u, step)
            for u in range(HEADS):
                for step in range(STEPS):
                    step_start(SEQS - 1, u, step)
                    if u * STEPS + step < GROUPS:
                        dense_pairs(SEQS - 1, u * STEPS + step)
                    step_end(SEQS - 1, u, step)
            back_end(SEQS - 1)


def kernel(**inputs):
    import concourse.bacc as _bacc
    from concourse.bass_utils import run_bass_kernel_spmd as _run

    a = {k: np.ascontiguousarray(v) for k, v in inputs.items()}

    def aug(w, b):
        return np.concatenate([w, b[None, :]], axis=0)

    arrays = {
        "x": a["x"], "emb2": a["L0_tok_emb_2"], "emb3": a["L0_tok_emb_3"], "emb4": a["L0_tok_emb_4"],
        "attn_w": np.stack([aug(a[f"L0_attn_W{c}"].T, a[f"L0_attn_b{c}"]) for c in "qkv"], axis=1),
        "wi_aug": aug(a["L0_ffn_Wi"].T, a["L0_ffn_bi"]),
        "route": a["L0_ffn_route_id"],
        "wr": a["L0_ffn_Wr"].transpose(3, 0, 1, 2), "br": a["L0_ffn_br"].transpose(2, 0, 1),
        "ws": a["L0_ffn_Ws"][:, 0].transpose(2, 0, 1), "bs": a["L0_ffn_bs"][:, 0].T,
        "wo_ffn": a["L0_ffn_Wo"].T, "bo": a["L0_ffn_bo"][None, :],
        "qkv_aug": aug(a["L1_attn_w_qkv"], a["L1_attn_b_qkv"]),
        "norm_gb": np.stack([a["L1_attn_norm_g"], a["L1_attn_norm_b"]], axis=1),
        "fc1_aug": aug(a["L1_attn_w_fc1"], a["L1_attn_b_fc1"]),
        "fc2": a["L1_attn_w_fc2"].reshape(2, MLP_HALF, DIM).transpose(1, 0, 2), "bfc2": a["L1_attn_b_fc2"][None, :],
        "wq_pk": a["L1_ffn_Wq_pk"], "pk_keys": a["L1_ffn_pk_keys"].transpose(0, 2, 3, 1), "wq": a["L1_ffn_Wq"],
        "kv_table": np.concatenate([a["L1_ffn_keys_table"], a["L1_ffn_values_table"]], axis=1),
        "wo": a["L1_ffn_Wo"].reshape(HEADS, DIM, DIM).transpose(1, 0, 2),
        "const": constants(), "sel": selections(), "key_no": key_numbers(),
    }
    arrays = {f"in_{k}": np.ascontiguousarray(v) for k, v in arrays.items()}
    nc = _bacc.Bacc("TRN2", target_bir_lowering=False, num_devices=1)
    args = [nc.dram_tensor(k, v.shape, mybir.dt.from_np(v.dtype), kind="ExternalInput").ap() for k, v in arrays.items()]
    args.append(nc.dram_tensor("out", (SEQS, TOK, DIM), F32, kind="ExternalOutput").ap())
    tower(nc, *args)
    r = _run(nc, [arrays], core_ids=[0])
    return r.results[0]["out"]
```
